# Optimizing a Trainium2 kernel written in Bass

```python
import numpy as np
import jax
import jax.numpy as jnp

def _softmax(x, axis=-1):
    return jax.nn.softmax(x, axis=axis)

def _gelu(x):
    return jax.nn.gelu(x, approximate=True)

def _silu(x):
    return jax.nn.silu(x)

def _sigmoid(x):
    return jax.nn.sigmoid(x)

def _layernorm(x, axis=-1, eps=1e-05):
    m = jnp.mean(x, axis=axis, keepdims=True)
    v = jnp.var(x, axis=axis, keepdims=True)
    return (x - m) / jnp.sqrt(v + eps)

def _scatter_add(tgt, idx, src, axis=0):
    return tgt.at[idx].add(src)

def _segment_sum(src, seg, n):
    return jax.ops.segment_sum(src, seg, n)
kernel_name = 'mk_gnn_resnorm_d4_gnn_r32_7d5563'

def setup_inputs(seed: int=0):
    np.random.seed(seed)
    _w = jnp.asarray

    def _rec_inputs():
        import jax
        import jax.numpy as jnp
        _gk = jax.random.key(seed)
        x = -0.0005207 + 1.001 * jax.random.normal(jax.random.fold_in(_gk, 1), (128, 512), jnp.float32)
        src = jax.random.randint(jax.random.fold_in(_gk, 2), (4096,), 0, 128, jnp.int32)
        dst = jnp.minimum((128 * jax.random.uniform(jax.random.fold_in(_gk, 3), (4096,)) ** 2.0).astype(jnp.int32), 4095)
        _o = jnp.argsort(dst, stable=True)
        src = src[_o]
        dst = dst[_o]
        edge_attr_64 = 0.000279952 + 1.00013 * jax.random.normal(jax.random.fold_in(_gk, 13), (4096, 64), jnp.float32)
        return (x, src, dst, edge_attr_64)
    x, src, dst, edge_attr_64 = _rec_inputs()

    def _L0_gnn_setup():
        import jax, jax.numpy as jnp
        import numpy as np
        N, E = (128, 4096)
        D_IN, D_OUT, H = (512, 512, 8)
        HEAD = D_OUT // H
        EPS = 1e-05

        def _layer_norm(x, g, b):
            m = jnp.mean(x, axis=-1, keepdims=True)
            v = jnp.mean(jnp.square(x - m), axis=-1, keepdims=True)
            return (x - m) * jax.lax.rsqrt(v + EPS) * g + b
        key = jax.random.key(seed)
        ks = jax.random.split(key, 16)
        s = 1.0 / np.sqrt(D_OUT)
        inp = {'x': jax.random.normal(ks[0], (N, D_IN), dtype=jnp.float32), 'edge_index': jax.random.randint(ks[1], (2, E), 0, N, dtype=jnp.int64), 'Wq': jax.random.normal(ks[2], (D_OUT, D_OUT), jnp.float32) * s, 'bq': jnp.zeros((D_OUT,), jnp.float32), 'Wk': jax.random.normal(ks[3], (D_OUT, D_OUT), jnp.float32) * s, 'bk': jnp.zeros((D_OUT,), jnp.float32), 'Wv': jax.random.normal(ks[4], (D_OUT, D_OUT), jnp.float32) * s, 'bv': jnp.zeros((D_OUT,), jnp.float32), 'Wo': jax.random.normal(ks[5], (D_OUT, D_OUT), jnp.float32) * s, 'bo': jnp.zeros((D_OUT,), jnp.float32), 'W1': jax.random.normal(ks[6], (D_OUT, 2 * D_OUT), jnp.float32) * s, 'b1': jnp.zeros((2 * D_OUT,), jnp.float32), 'W2': jax.random.normal(ks[7], (2 * D_OUT, D_OUT), jnp.float32) * (1.0 / np.sqrt(2 * D_OUT)), 'b2': jnp.zeros((D_OUT,), jnp.float32), 'g1': jnp.ones((D_OUT,), jnp.float32), 'be1': jnp.zeros((D_OUT,), jnp.float32), 'g2': jnp.ones((D_OUT,), jnp.float32), 'be2': jnp.zeros((D_OUT,), jnp.float32)}
        return inp
    _L0_gnn_all = _L0_gnn_setup()
    _L0_gnn_in = {k: v for k, v in _L0_gnn_all.items() if k in ('Wq', 'bq', 'Wk', 'bk', 'Wv', 'bv', 'Wo', 'bo', 'W1', 'b1', 'W2', 'b2', 'g1', 'be1', 'g2', 'be2')}
    del _L0_gnn_all

    def _L1_gnn_setup():
        import jax, jax.numpy as jnp
        import numpy as np
        N_NODES = 625
        N_EDGES = 10000
        HIDDEN = 512
        EDGE_DIM = 64
        LN_EPS = 1e-05

        def mish(x):
            return x * jnp.tanh(jax.nn.softplus(x))
        key = jax.random.key(seed)
        ks = jax.random.split(key, 8)
        s = lambda fan_in: 1.0 / np.sqrt(fan_in)
        return {'x': jax.random.normal(ks[0], (N_NODES, HIDDEN), dtype=jnp.float32), 'edge_index': jax.random.randint(ks[1], (2, N_EDGES), 0, N_NODES, dtype=jnp.int64), 'edge_attr': jax.random.normal(ks[2], (N_EDGES, EDGE_DIM), dtype=jnp.float32), 'W1': jax.random.normal(ks[3], (2 * HIDDEN + EDGE_DIM, HIDDEN), dtype=jnp.float32) * s(2 * HIDDEN + EDGE_DIM), 'b1': jnp.zeros((HIDDEN,), dtype=jnp.float32), 'W2': jax.random.normal(ks[4], (HIDDEN, HIDDEN), dtype=jnp.float32) * s(HIDDEN), 'b2': jnp.zeros((HIDDEN,), dtype=jnp.float32), 'W3': jax.random.normal(ks[5], (2 * HIDDEN, HIDDEN), dtype=jnp.float32) * s(2 * HIDDEN), 'b3': jnp.zeros((HIDDEN,), dtype=jnp.float32), 'W4': jax.random.normal(ks[6], (HIDDEN, HIDDEN), dtype=jnp.float32) * s(HIDDEN), 'b4': jnp.zeros((HIDDEN,), dtype=jnp.float32), 'gamma': jnp.ones((HIDDEN,), dtype=jnp.float32), 'beta': jnp.zeros((HIDDEN,), dtype=jnp.float32)}
    _L1_gnn_all = _L1_gnn_setup()
    _L1_gnn_in = {k: v for k, v in _L1_gnn_all.items() if k in ('W1', 'b1', 'W2', 'b2', 'W3', 'b3', 'W4', 'b4', 'gamma', 'beta')}
    del _L1_gnn_all

    def _L2_gnn_setup():
        import jax, jax.numpy as jnp
        import numpy as np
        N = 3125
        IN_C = 512
        HID = 128
        OUT_C = 512
        E = 100000

        def _gcn_conv(x, W, b, src, dst, n):
            h = x @ W
            loop = jnp.arange(n, dtype=src.dtype)
            src2 = jnp.concatenate([src, loop])
            dst2 = jnp.concatenate([dst, loop])
            deg = jax.ops.segment_sum(jnp.ones_like(dst2, dtype=h.dtype), dst2, num_segments=n)
            dinv = jnp.where(deg > 0, jax.lax.rsqrt(deg), 0.0)
            norm = dinv[src2] * dinv[dst2]
            msgs = h[src2] * norm[:, None]
            out = jax.ops.segment_sum(msgs, dst2, num_segments=n)
            return out + b
        key = jax.random.key(seed)
        k1, k2, k3, k4 = jax.random.split(key, 4)
        z = jax.random.normal(k1, (N, IN_C), dtype=jnp.float32)
        edge_index = jax.random.randint(k2, (2, E), 0, N, dtype=jnp.int64)
        W1 = jax.random.normal(k3, (IN_C, HID), dtype=jnp.float32) * (1.0 / np.sqrt(IN_C))
        b1 = jnp.zeros((HID,), dtype=jnp.float32)
        W2 = jax.random.normal(k4, (HID, OUT_C), dtype=jnp.float32) * (1.0 / np.sqrt(HID))
        b2 = jnp.zeros((OUT_C,), dtype=jnp.float32)
        return {'z': z, 'edge_index': edge_index, 'W1': W1, 'b1': b1, 'W2': W2, 'b2': b2}
    _L2_gnn_all = _L2_gnn_setup()
    _L2_gnn_in = {k: v for k, v in _L2_gnn_all.items() if k in ('W1', 'b1', 'W2', 'b2')}
    del _L2_gnn_all

    def _L3_gnn_setup():
        import jax, jax.numpy as jnp
        import numpy as np
        N_NODES = 10000
        N_EDGES = 5000
        IN_DIM = 512
        OUT_DIM = 512
        LN_EPS = 1e-05
        key = jax.random.key(seed)
        k_x, k_src, k_ws, k_wn = jax.random.split(key, 4)
        x = jax.random.normal(k_x, (N_NODES, IN_DIM), dtype=jnp.float32)
        edge_src = jax.random.randint(k_src, (N_EDGES,), 0, N_NODES, dtype=jnp.int32)
        edge_dst = jnp.repeat(jnp.arange(N_NODES, dtype=jnp.int32), N_EDGES // N_NODES)
        deg = jnp.full((N_NODES,), float(N_EDGES // N_NODES), dtype=jnp.float32)
        scale = 1.0 / np.sqrt(IN_DIM)
        W_self = jax.random.normal(k_ws, (OUT_DIM, IN_DIM), dtype=jnp.float32) * scale
        W_neigh = jax.random.normal(k_wn, (OUT_DIM, IN_DIM), dtype=jnp.float32) * scale
        bias = jnp.zeros((OUT_DIM,), dtype=jnp.float32)
        gamma = jnp.ones((OUT_DIM,), dtype=jnp.float32)
        beta = jnp.zeros((OUT_DIM,), dtype=jnp.float32)
        return {'x': x, 'edge_src': edge_src, 'edge_dst': edge_dst, 'deg': deg, 'W_self': W_self, 'W_neigh': W_neigh, 'bias': bias, 'gamma': gamma, 'beta': beta}
    _L3_gnn_all = _L3_gnn_setup()
    _L3_gnn_in = {k: v for k, v in _L3_gnn_all.items() if k in ('W_self', 'W_neigh', 'bias', 'gamma', 'beta')}
    del _L3_gnn_all
    return {'x': x, 'src': src, 'dst': dst, 'edge_attr_64': edge_attr_64, 'L0_gnn_Wq': _L0_gnn_in['Wq'], 'L0_gnn_bq': _L0_gnn_in['bq'], 'L0_gnn_Wk': _L0_gnn_in['Wk'], 'L0_gnn_bk': _L0_gnn_in['bk'], 'L0_gnn_Wv': _L0_gnn_in['Wv'], 'L0_gnn_bv': _L0_gnn_in['bv'], 'L0_gnn_Wo': _L0_gnn_in['Wo'], 'L0_gnn_bo': _L0_gnn_in['bo'], 'L0_gnn_W1': _L0_gnn_in['W1'], 'L0_gnn_b1': _L0_gnn_in['b1'], 'L0_gnn_W2': _L0_gnn_in['W2'], 'L0_gnn_b2': _L0_gnn_in['b2'], 'L0_gnn_g1': _L0_gnn_in['g1'], 'L0_gnn_be1': _L0_gnn_in['be1'], 'L0_gnn_g2': _L0_gnn_in['g2'], 'L0_gnn_be2': _L0_gnn_in['be2'], 'L1_gnn_W1': _L1_gnn_in['W1'], 'L1_gnn_b1': _L1_gnn_in['b1'], 'L1_gnn_W2': _L1_gnn_in['W2'], 'L1_gnn_b2': _L1_gnn_in['b2'], 'L1_gnn_W3': _L1_gnn_in['W3'], 'L1_gnn_b3': _L1_gnn_in['b3'], 'L1_gnn_W4': _L1_gnn_in['W4'], 'L1_gnn_b4': _L1_gnn_in['b4'], 'L1_gnn_gamma': _L1_gnn_in['gamma'], 'L1_gnn_beta': _L1_gnn_in['beta'], 'L2_gnn_W1': _L2_gnn_in['W1'], 'L2_gnn_b1': _L2_gnn_in['b1'], 'L2_gnn_W2': _L2_gnn_in['W2'], 'L2_gnn_b2': _L2_gnn_in['b2'], 'L3_gnn_W_self': _L3_gnn_in['W_self'], 'L3_gnn_W_neigh': _L3_gnn_in['W_neigh'], 'L3_gnn_bias': _L3_gnn_in['bias'], 'L3_gnn_gamma': _L3_gnn_in['gamma'], 'L3_gnn_beta': _L3_gnn_in['beta']}

def reference(x, src, dst, edge_attr_64, L0_gnn_Wq, L0_gnn_bq, L0_gnn_Wk, L0_gnn_bk, L0_gnn_Wv, L0_gnn_bv, L0_gnn_Wo, L0_gnn_bo, L0_gnn_W1, L0_gnn_b1, L0_gnn_W2, L0_gnn_b2, L0_gnn_g1, L0_gnn_be1, L0_gnn_g2, L0_gnn_be2, L1_gnn_W1, L1_gnn_b1, L1_gnn_W2, L1_gnn_b2, L1_gnn_W3, L1_gnn_b3, L1_gnn_W4, L1_gnn_b4, L1_gnn_gamma, L1_gnn_beta, L2_gnn_W1, L2_gnn_b1, L2_gnn_W2, L2_gnn_b2, L3_gnn_W_self, L3_gnn_W_neigh, L3_gnn_bias, L3_gnn_gamma, L3_gnn_beta):
    import jax
    import jax.numpy as jnp

    def _L0_gnn_ref(x, edge_index, Wq, bq, Wk, bk, Wv, bv, Wo, bo, W1, b1, W2, b2, g1, be1, g2, be2):
        import jax, jax.numpy as jnp
        import numpy as np
        N, E = (128, 4096)
        D_IN, D_OUT, H = (512, 512, 8)
        HEAD = D_OUT // H
        EPS = 1e-05

        def _layer_norm(x, g, b):
            m = jnp.mean(x, axis=-1, keepdims=True)
            v = jnp.mean(jnp.square(x - m), axis=-1, keepdims=True)
            return (x - m) * jax.lax.rsqrt(v + EPS) * g + b
        q = (x @ Wq + bq).reshape(N, H, HEAD)
        k = (x @ Wk + bk).reshape(N, H, HEAD)
        v = (x @ Wv + bv).reshape(N, H, HEAD)
        scores = jnp.einsum('nhd,mhd->nhm', q, k) / np.sqrt(HEAD)
        adj = jnp.zeros((N, N), jnp.float32).at[edge_index[0], edge_index[1]].set(1.0)
        scores = jnp.where(adj[:, None, :] == 0, -1000000000.0, scores)
        attn = jax.nn.softmax(scores, axis=1)
        attn_out = jnp.einsum('nhm,mhd->nhd', attn, v).reshape(N, D_OUT)
        attn_out = attn_out @ Wo + bo
        h1 = _layer_norm(x + attn_out, g1, be1)
        ff = jax.nn.relu(h1 @ W1 + b1) @ W2 + b2
        return _layer_norm(h1 + ff, g2, be2)

    def _L1_gnn_ref(x, edge_index, edge_attr, W1, b1, W2, b2, W3, b3, W4, b4, gamma, beta):
        import jax, jax.numpy as jnp
        import numpy as np
        N_NODES = 625
        N_EDGES = 10000
        HIDDEN = 512
        EDGE_DIM = 64
        LN_EPS = 1e-05

        def mish(x):
            return x * jnp.tanh(jax.nn.softplus(x))
        src, dst = (edge_index[0], edge_index[1])
        edge_feat = jnp.concatenate([x[src], x[dst], edge_attr], axis=-1)
        h = mish(edge_feat @ W1 + b1)
        messages = mish(h @ W2 + b2)
        agg = jax.ops.segment_sum(messages, dst, num_segments=x.shape[0])
        u = mish(jnp.concatenate([x, agg], axis=-1) @ W3 + b3)
        out = u @ W4 + b4
        y = x + out
        mu = jnp.mean(y, axis=-1, keepdims=True)
        var = jnp.mean(jnp.square(y - mu), axis=-1, keepdims=True)
        return (y - mu) * jax.lax.rsqrt(var + LN_EPS) * gamma + beta

    def _L2_gnn_ref(z, edge_index, W1, b1, W2, b2):
        import jax, jax.numpy as jnp
        import numpy as np
        N = 3125
        IN_C = 512
        HID = 128
        OUT_C = 512
        E = 100000

        def _gcn_conv(x, W, b, src, dst, n):
            h = x @ W
            loop = jnp.arange(n, dtype=src.dtype)
            src2 = jnp.concatenate([src, loop])
            dst2 = jnp.concatenate([dst, loop])
            deg = jax.ops.segment_sum(jnp.ones_like(dst2, dtype=h.dtype), dst2, num_segments=n)
            dinv = jnp.where(deg > 0, jax.lax.rsqrt(deg), 0.0)
            norm = dinv[src2] * dinv[dst2]
            msgs = h[src2] * norm[:, None]
            out = jax.ops.segment_sum(msgs, dst2, num_segments=n)
            return out + b
        src, dst = (edge_index[0], edge_index[1])
        h = jax.nn.relu(_gcn_conv(z, W1, b1, src, dst, z.shape[0]))
        out = _gcn_conv(h, W2, b2, src, dst, z.shape[0])
        return out

    def _L3_gnn_ref(x, edge_src, edge_dst, deg, W_self, W_neigh, bias, gamma, beta):
        import jax, jax.numpy as jnp
        import numpy as np
        N_NODES = 10000
        N_EDGES = 5000
        IN_DIM = 512
        OUT_DIM = 512
        LN_EPS = 1e-05
        n = x.shape[0]
        h_self = jnp.einsum('nd,od->no', x, W_self)
        neigh_sum = jax.ops.segment_sum(x[edge_src], edge_dst, num_segments=n)
        neigh_mean = neigh_sum / jnp.maximum(deg, 1.0)[:, None]
        h_neigh = jnp.einsum('nd,od->no', neigh_mean, W_neigh)
        h = h_self + h_neigh + bias
        mu = jnp.mean(h, axis=-1, keepdims=True)
        var = jnp.mean(jnp.square(h - mu), axis=-1, keepdims=True)
        h = (h - mu) * jax.lax.rsqrt(var + LN_EPS)
        return h * gamma + beta
    edge_index = jnp.stack([src, dst])
    deg = jnp.maximum(jax.ops.segment_sum(jnp.ones(dst.shape, jnp.float32), dst, num_segments=128), 1.0)
    x = _layernorm(x + _L0_gnn_ref(x, edge_index, L0_gnn_Wq, L0_gnn_bq, L0_gnn_Wk, L0_gnn_bk, L0_gnn_Wv, L0_gnn_bv, L0_gnn_Wo, L0_gnn_bo, L0_gnn_W1, L0_gnn_b1, L0_gnn_W2, L0_gnn_b2, L0_gnn_g1, L0_gnn_be1, L0_gnn_g2, L0_gnn_be2), axis=-1)
    x = _layernorm(x + _L1_gnn_ref(x, edge_index, edge_attr_64, L1_gnn_W1, L1_gnn_b1, L1_gnn_W2, L1_gnn_b2, L1_gnn_W3, L1_gnn_b3, L1_gnn_W4, L1_gnn_b4, L1_gnn_gamma, L1_gnn_beta), axis=-1)
    x = _layernorm(x + _L2_gnn_ref(x, edge_index, L2_gnn_W1, L2_gnn_b1, L2_gnn_W2, L2_gnn_b2), axis=-1)
    x = _layernorm(x + _L3_gnn_ref(x, src, dst, deg, L3_gnn_W_self, L3_gnn_W_neigh, L3_gnn_bias, L3_gnn_gamma, L3_gnn_beta), axis=-1)
    return x

_drawn_inputs = setup_inputs


def setup_inputs(seed=0):
    import zlib

    import numpy as np

    out = dict(_drawn_inputs(seed))
    spreads = {'L0_gnn_bq': (0.0, 0.521),
     'L0_gnn_bk': (0.0, 0.571),
     'L0_gnn_bv': (0.0, 0.1),
     'L0_gnn_bo': (0.0, 0.1),
     'L0_gnn_b1': (0.0, 0.1),
     'L0_gnn_b2': (0.0, 0.1),
     'L0_gnn_g1': (1.0, 0.2),
     'L0_gnn_be1': (0.0, 0.1),
     'L0_gnn_g2': (1.0, 0.2),
     'L0_gnn_be2': (0.0, 0.1),
     'L1_gnn_b1': (0.0, 0.1),
     'L1_gnn_b2': (0.0, 0.1),
     'L1_gnn_b3': (0.0, 0.651),
     'L1_gnn_b4': (0.0, 0.439),
     'L1_gnn_gamma': (1.0, 0.2),
     'L1_gnn_beta': (0.0, 0.1),
     'L2_gnn_b1': (0.0, 0.1),
     'L2_gnn_b2': (0.0, 0.1),
     'L3_gnn_bias': (0.0, 0.1),
     'L3_gnn_gamma': (1.0, 0.2),
     'L3_gnn_beta': (0.0, 0.1)}
    factors = {}
    for name, (base, spread) in spreads.items():
        noise = np.random.default_rng([zlib.crc32(name.encode()), seed]).standard_normal(out[name].shape)
        drawn = base * np.exp(spread * noise) if base else spread * noise
        out[name] = jnp.asarray(drawn.astype(out[name].dtype))
    for name, factor in factors.items():
        out[name] = (out[name] * factor).astype(out[name].dtype)
    return out
```

```python
import concourse.bass as bass
from concourse import mybir
from contextlib import ExitStack

F32 = mybir.dt.float32
F32R = mybir.dt.float32r
BF16 = mybir.dt.bfloat16
I32 = mybir.dt.int32
ALU = mybir.AluOpType
ACT = mybir.ActivationFunctionType
AX = mybir.AxisListType

P = 128
N = 128
D = 512
KC = D // P
E = 4096
ET = E // P
EDIM = 64
HEADS = 8
HEAD = D // HEADS
FF = 2 * D
FC = FF // P
HID2 = 128
EPS = 1e-5
GT = 4
GE = GT * P
G = E // GE
LAG2 = 2
LAG3 = 4
HALF = KC * GE
TINY = 2.0 ** -63

ROWS = ["L0_gnn_bv", "L0_gnn_bo", "L0_gnn_g1", "L0_gnn_be1", "L0_gnn_b2", "L0_gnn_g2", "L0_gnn_be2",
        "L1_gnn_b2", "L1_gnn_b4", "L1_gnn_gamma", "L1_gnn_beta", "L2_gnn_b2",
        "L3_gnn_bias", "L3_gnn_gamma", "L3_gnn_beta"]
COLS = [("L0_gnn_bq", KC), ("L0_gnn_bk", KC), ("L0_gnn_b1", FC), ("L1_gnn_b1", KC), ("L1_gnn_b3", KC)]


def gnn_kernel(nc, a, out):
    ctx = ExitStack()
    with ctx:
        def sb(name, shape, dt=F32):
            return ctx.enter_context(nc.sbuf_tensor(name, shape, dt))

        def sem(name):
            return ctx.enter_context(nc.semaphore(name))

        Z = sb("Z", [P, 2, 2 * HALF])
        T = sb("T", [P, 2 * HALF])
        Dg = sb("Dg", [P, GT, N], F32R)
        Chi = sb("Chi", [P, D], F32R)
        Clo = sb("Clo", [P, D], F32R)
        rows = sb("rows", [P, 8, D])
        vecs = sb("vecs", [24, P])
        cols = sb("cols", [P, 24])
        b1g = sb("b1g", [P, HID2])
        xs = sb("xs", [P, D])
        xT = sb("xT", [P, KC, N])
        xw = sb("xw", [P, D])
        y = sb("y", [P, D])
        iota_row = sb("iota_row", [P, P])
        iota_col = sb("iota_col", [P, 1])
        ident = sb("ident", [P, P])
        dcol = sb("dcol", [P, ET], I32)
        scol = sb("scol", [P, ET], I32)
        Ahat = sb("Ahat", [P, N])
        Cn = sb("Cn", [P, N])
        CTs = sb("CTs", [P, N])
        mask = sb("mask", [P, N])
        small = sb("small", [P, 16])
        stats = sb("stats", [P, 6])
        mv = sb("mv", [P, 2])
        rstd = sb("rstd", [P, 1])
        mhalf = sb("mhalf", [P, 1])
        tiny = sb("tiny", [P, 1])
        small_n = sb("small_n", [P, 2, N])

        Z0, Z1 = Z[:, 0, :], Z[:, 1, :]

        def chunks(v, k):
            return v.rearrange("p (c n) -> p c n", c=k)

        def stage(*tensors):
            with ExitStack() as st:
                made = []
                for name, words, dt in tensors:
                    t = st.enter_context(nc.sbuf_tensor(name, [P, words], dt))
                    made.append(t[:, :])
            return [t for t, (name, _, _) in zip(made, tensors) if not name.startswith("pad")]

        W = KC * D
        Wq, Wk, Wv, Wo, MA, MB, Dbf, Sbf, ea_raw, idrow0 = stage(
            ("Wq", W, F32), ("Wk", W, F32), ("Wv", W, F32), ("Wo", W, F32), ("MA", W, F32), ("MB", W, F32),
            ("Dbf", 2 * W, BF16), ("Sbf", 2 * W, BF16), ("ea_raw", W, F32), ("pad0", 2 * E, F32), ("idrow", E, I32))
        Hhi, Hlo, Mhi, Mlo, W2hi, W2lo, Ahi, Alo, Bhi, Blo, ST, DT, EAT = stage(
            ("Hhi", 2 * W, F32R),
            ("Hlo", 2 * W, F32R),
            ("Mhi", W, F32R), ("Mlo", W, F32R),
            ("W2hi", W, F32R), ("W2lo", W, F32R),
            ("Ahi", D, F32R), ("Alo", D, F32R), ("Bhi", D, F32R), ("Blo", D, F32R),
            ("ST", E, F32R), ("DT", E, F32R),
            ("EAT", E, F32R))
        WsT, WnT, tail, WsR, WnR, W4, G1, G2, W3 = stage(
            ("WsT", W, F32), ("WnT", W, F32), ("tail", 2 * W, F32), ("pad1", 5 * W, F32),
            ("WsR", W, F32), ("WnR", W, F32), ("W4", W, F32), ("G1", D, F32), ("G2", D, F32),
            ("pad2", 2 * D, F32), ("W3", 2 * W, F32))
        stage_bytes = ctx.enter_context(nc.sbuf_tensor("stages", [P, 15 * W], F32))

        Wq, Wk, Wv, Wo, W4, WsR, WnR, WsT, WnT, G1 = (chunks(w, KC) for w in (Wq, Wk, Wv, Wo, W4, WsR, WnR, WsT, WnT, G1))
        W2hi, W2lo = chunks(W2hi, KC), chunks(W2lo, KC)
        W3 = chunks(W3, 2 * KC)
        Hhi, Hlo = (h.rearrange("p (a k n) -> p a k n", a=2, k=KC) for h in (Hhi, Hlo))
        Mhi, Mlo = chunks(Mhi, GT), chunks(Mlo, GT)
        Dbf, Sbf = chunks(Dbf, ET), chunks(Sbf, ET)
        W2raw = chunks(ea_raw, KC)
        ea_raw = chunks(ea_raw, ET)
        F1 = chunks(T[:, :], KC)
        F2 = chunks(Z0, FC)
        src_bc, dst_bc = Z0.bitcast(I32), Z1.bitcast(I32)
        EAs = chunks(Z0, ET)
        W1ab = chunks(Z1, 2 * KC)
        qT = chunks(MA[:, 0:D], KC)
        kT = chunks(MA[:, D:2 * D], KC)
        v_sb = MA[:, 2 * D:3 * D]
        aoT = chunks(MA[:, 3 * D:4 * D], KC)
        attn = MB[:, 0:2 * D].rearrange("p (o j n) -> p o j n", o=2, j=KC)
        ffT = chunks(MB[:, 2 * D:4 * D], FC)
        Wc_raw = y
        idrow = [idrow0[0:1, :], T[0:1, :].bitcast(I32)]
        rowvec = sb("rowvec", [1, 2, D])
        ux = tail[:, 0:D]
        zu = tail[:, D:2 * D]
        tu = tail[:, 2 * D:3 * D]
        uT = chunks(tail[:, 3 * D:4 * D], KC)
        aggT = chunks(tail[:, 4 * D:5 * D], KC)
        agg_sb = tail[:, 5 * D:6 * D]
        h0g = tail[:, 6 * D:6 * D + HID2]
        r1g = tail[:, 6 * D + HID2:6 * D + 2 * HID2]
        p1g = tail[:, 6 * D + 2 * HID2:6 * D + 3 * HID2]
        nmT = chunks(tail[:, 7 * D:8 * D], KC)

        bank = [ctx.enter_context(nc.psum_tensor(f"bank{i}", [P, D], F32)) for i in range(8)]
        AGG, ST1, ST2, MISC = bank[0], bank[1:3], bank[3:7], bank[7]

        def quarter(b, j):
            return b[:, P * j:P * (j + 1)]

        col = {}
        at = 0
        for name, k in COLS:
            col[name] = at
            at += k
        slot = {name: i for i, name in enumerate(ROWS[:8])}
        again = ROWS[8:]
        slot.update({name: i for i, name in enumerate(again)})

        S = {}
        for name in ("x_in ids_in vecs_in ea_in wq_in wk_in wv_in wo_in f1_in f2_in w1ab_in wc_in w2_in w3_in w4_in g_in ws_in wn_in b1g_in "
                     "out_stored consts ident_ready x_transposed xT_ready cols_done cols_ready q_done k_done v_done "
                     "qk_ready v_ready onehot_bf ct_done ct_read scores_done scores_read s_centred exp_done attn_ready ao_done ao_ready wo_done "
                     "stat_ready rstd_ready nx_ready nT_done nT_ready f1_done ff_ready f2_done "
                     "ids_row bc_ready st_ready ea_hi ea_split ea_T ea_Tready w2_hi w2_split c_split ab_done ab_ready "
                     "graphT_ready graphT_done graph_ready deg_ready dinv_ready "
                     "z1_done z1_read z2_done z2_read sig1 sig2 log_done tanh1 tanh2 h_mul h_hi h_lo m_mul m_hi m_lo m_oh agg_done st1_all "
                     "ux_done ux_ready agg_ready aggT_done aggT_ready u_done zu_ready u_act u_ready o_done "
                     "g0_done g0_ready g1_done g1_ready g2_done g2_ready g3_done nm_done nm_ready l3_done wt_done wt_ready y_final "
                     "dve_chain act_chain pool_chain").split():
            S[name] = sem(name)
        row_in = [sem(f"row_in{i}") for i in range(2)]
        row_out = sem("row_out")

        block = ctx.enter_context(nc.Block())

        def w_view(w):
            return w.rearrange("(c p) n -> p c n", p=P)

        def hop(eng, name):
            n = [0]

            def link(ins):
                n[0] += 1
                ins.then_inc(S[name], 1)
                eng.wait_ge(S[name], n[0])
            return link

        def logs(s, part):
            return min(s, G) + max(0, s - LAG2) + (2 if part and s < G else 1)

        @block.sync
        def _(sp):
            sp.dma_start(scol[:, :], a["src"].rearrange("(p t) -> p t", p=P)).then_inc(S["ids_in"], 16)
            sp.dma_start(dcol[:, :], a["dst"].rearrange("(p t) -> p t", p=P)).then_inc(S["ids_in"], 16)
            sp.dma_start(xs[:, :], a["x"]).then_inc(S["x_in"], 16)
            sp.dma_start(Wq, w_view(a["L0_gnn_Wq"])).then_inc(S["wq_in"], 16)
            sp.dma_start(idrow[0], a["src"].rearrange("(o n) -> o n", o=1)).then_inc(S["ids_row"], 16)
            sp.dma_start(idrow[1], a["dst"].rearrange("(o n) -> o n", o=1)).then_inc(S["ids_row"], 16)
            sp.dma_start(Wk, w_view(a["L0_gnn_Wk"])).then_inc(S["wk_in"], 16)
            sp.dma_start(Wv, w_view(a["L0_gnn_Wv"])).then_inc(S["wv_in"], 16)
            sp.dma_start(ea_raw[:, :, :], a["edge_attr_64"].rearrange("(p t) n -> p t n", p=P)).then_inc(S["ea_in"], 16)
            sp.dma_start(Wo, w_view(a["L0_gnn_Wo"])).then_inc(S["wo_in"], 16)
            sp.wait_ge(S["bc_ready"], 2)
            sp.dma_start(F1, w_view(a["L0_gnn_W1"])).then_inc(S["f1_in"], 16)
            sp.wait_ge(S["st_ready"], 2)
            sp.dma_start(W1ab, w_view(a["L1_gnn_W1"][0:2 * D, :])).then_inc(S["w1ab_in"], 16)
            sp.wait_ge(S["ea_split"], 1)
            sp.dma_start(W2raw, w_view(a["L1_gnn_W2"])).then_inc(S["w2_in"], 16)
            sp.wait_ge(S["ea_T"], 8)
            sp.dma_start(F2, w_view(a["L0_gnn_W2"])).then_inc(S["f2_in"], 16)
            sp.wait_ge(S["z1_done"], KC * G)
            sp.dma_start(W3, w_view(a["L1_gnn_W3"])).then_inc(S["w3_in"], 16)
            sp.dma_start(W4, w_view(a["L1_gnn_W4"])).then_inc(S["w4_in"], 16)
            sp.dma_start(G1, w_view(a["L2_gnn_W1"])).then_inc(S["g_in"], 16)
            sp.dma_start(G2, a["L2_gnn_W2"]).then_inc(S["g_in"], 16)
            sp.dma_start(WsR, w_view(a["L3_gnn_W_self"])).then_inc(S["ws_in"], 16)
            sp.dma_start(WnR, w_view(a["L3_gnn_W_neigh"])).then_inc(S["wn_in"], 16)
            sp.wait_ge(S["y_final"], 1)
            sp.dma_start(out, y[:, :]).then_inc(S["out_stored"], 16)
            sp.wait_ge(S["out_stored"], 16)

        @block.gpsimd
        def _(pool):
            chain = hop(pool, "pool_chain")
            pool.iota(iota_row[:, :], pattern=[[1, P]], base=0, channel_multiplier=0,
                      allow_small_or_imprecise_dtypes=True).then_inc(S["consts"], 1)
            pool.iota(iota_col[:, :], pattern=[[0, 1]], base=0, channel_multiplier=1,
                      allow_small_or_imprecise_dtypes=True).then_inc(S["consts"], 1)
            pool.memset(mhalf[:, :], -0.5).then_inc(S["consts"], 1)
            pool.wait_ge(S["consts"], 3)

            def row(i):
                pool.wait_ge(row_in[i % 2], 16 * (i // 2 + 1))
                pool.partition_broadcast(rows[:, slot[ROWS[i]], :], rowvec[0:1, i % 2, :]).then_inc(row_out, 1)

            def inverse_root(k, src, dst, ready, signal):
                pool.wait_ge(ready, k)
                pool.tensor_tensor(dst, src, mhalf[:, :], ALU.pow).then_inc(signal, 1)

            norms = [0]

            def norm():
                norms[0] += 1
                inverse_root(norms[0], mv[:, 1:2], rstd[:, :], S["stat_ready"], S["rstd_ready"])

            row(0)
            row(1)
            pool.wait_ge(S["ids_row"], 32)
            pool.partition_broadcast(dst_bc, idrow[1]).then_inc(S["bc_ready"], 1)
            pool.partition_broadcast(src_bc, idrow[0]).then_inc(S["bc_ready"], 1)
            inverse_root(1, small[:, 1:2], small[:, 2:3], S["deg_ready"], S["dinv_ready"])
            for i in range(2, 8):
                row(i)
            norm()
            pool.wait_ge(S["ea_hi"], 1)
            pool.tensor_tensor(EAs[:, :, EDIM:], ea_raw[:, :, :], EAs[:, :, 0:EDIM], ALU.subtract).then_inc(S["ea_split"], 1)
            pool.wait_ge(S["w2_hi"], 1)
            pool.tensor_tensor(W2lo[:, :, :], W2raw, W2hi.bitcast(F32), ALU.subtract).then_inc(S["w2_split"], 1)
            norm()
            norm()
            pool.wait_ge(S["nx_ready"], 3)
            for i in range(8, 15):
                row(i)
            for s in range(G + LAG2):
                if s < G:
                    pool.wait_ge(S["h_hi"], s + 1)
                    hl = Hlo[:, s % 2, :, :].rearrange("p k n -> p (k n)")
                    hh = Hhi[:, s % 2, :, :].rearrange("p k n -> p (k n)").bitcast(F32)
                    pool.tensor_tensor(hl, Z[:, s % 2, 0:HALF], hh, ALU.subtract).then_inc(S["h_lo"], 1)
                if s >= LAG2:
                    pool.wait_ge(S["m_hi"], s - LAG2 + 1)
                    pool.tensor_tensor(Mlo[:, :, :].rearrange("p t n -> p (t n)"), Z[:, s % 2, HALF:],
                                       Mhi[:, :, :].rearrange("p t n -> p (t n)").bitcast(F32),
                                       ALU.subtract).then_inc(S["m_lo"], 1)
            for _ in range(5):
                norm()

        @block.scalar
        def _(act):
            for i in range(2):
                act.dma_start(rowvec[0:1, i, :], a[ROWS[i]].rearrange("(o n) -> o n", o=1)).then_inc(row_in[i], 16)
            for name, k in COLS:
                act.dma_start(vecs[col[name]:col[name] + k, :], a[name].rearrange("(k p) -> k p", p=P)).then_inc(S["vecs_in"], 16)
            act.dma_start(b1g[:, :], a["L2_gnn_b1"].rearrange("(o n) -> o n", o=1).to_broadcast([P, HID2])).then_inc(S["b1g_in"], 16)
            for h in range(2):
                act.dma_start(Wc_raw[EDIM * h:EDIM * (h + 1), :], a["L1_gnn_W1"][2 * D:, :]).then_inc(S["wc_in"], 16)

            def load_rows(lo, hi):
                for i in range(lo, hi):
                    act.wait_ge(row_out, i - 1)
                    act.dma_start(rowvec[0:1, i % 2, :], a[ROWS[i]].rearrange("(o n) -> o n", o=1)).then_inc(row_in[i % 2], 16)

            def bias_out(dst, src, name, j, func=ACT.Identity):
                return act.activation(dst, src, func, bias=cols[:, col[name] + j:col[name] + j + 1])

            load_rows(2, 4)
            act.wait_ge(S["cols_ready"], 1)
            act.wait_ge(S["q_done"], 1)
            for j in range(KC):
                bias_out(qT[:, j, :], quarter(bank[2], j), "L0_gnn_bq", j).then_inc(S["qk_ready"], 1)
            act.wait_ge(S["k_done"], 1)
            for j in range(KC):
                bias_out(kT[:, j, :], quarter(bank[3], j), "L0_gnn_bk", j).then_inc(S["qk_ready"], 1)
            load_rows(4, 8)
            act.wait_ge(S["ea_in"], 16)
            act.wait_ge(S["s_centred"], 1)
            act.activation(attn.rearrange("p o j n -> p (o j n)"), attn.rearrange("p o j n -> p (o j n)"), ACT.Exp,
                           scale=float(HEAD) ** -0.5).then_inc(S["exp_done"], 1)
            act.wait_ge(S["st_ready"], 2)
            act.activation(EAs[:, :, 0:EDIM].bitcast(F32R), ea_raw[:, :, :], ACT.Copy).then_inc(S["ea_hi"], 1)
            act.wait_ge(S["ao_done"], 1)
            act.activation(aoT.rearrange("p c n -> p (c n)"), bank[2][:, :], ACT.Copy).then_inc(S["ao_ready"], 1)
            for q in range(ET // 4):
                act.wait_ge(S["ea_T"], q + 1)
                act.activation(EAT[:, 4 * P * q:4 * P * (q + 1)], bank[5 + q % 2][:, :], ACT.Copy).then_inc(S["ea_Tready"], 1)
            for i in range(4):
                act.wait_ge(S["f1_done"], i + 1)
                for j in (2 * i, 2 * i + 1):
                    bias_out(ffT[:, j, :], quarter((bank[2], bank[4], bank[5], bank[6])[i], j % 2), "L0_gnn_b1", j,
                             ACT.Relu).then_inc(S["ff_ready"], 1)
            act.wait_ge(S["w2_in"], 16)
            act.wait_ge(S["graph_ready"], 2)
            act.activation(W2hi[:, :, :], W2raw, ACT.Copy).then_inc(S["w2_hi"], 1)
            load_rows(8, 15)
            for s in range(G + LAG2):
                first, second = s < G, s >= LAG2
                z = Z[:, s % 2, :]
                lo, hi = (0 if first else HALF), (2 * HALF if second else HALF)
                if first:
                    act.wait_ge(S["z1_read"], KC * (s + 1))
                    if s >= 1:
                        act.wait_ge(S["h_mul"], 2 * s)
                    act.activation(T[:, 0:HALF], z[:, 0:HALF], ACT.Sigmoid, scale=-1.0).then_inc(S["sig1"], 1)
                if second:
                    for h in range(2):
                        act.wait_ge(S["z2_read"], GT * (s - LAG2) + 2 * (h + 1))
                        if s > LAG2:
                            act.wait_ge(S["m_mul"], 2 * (s - LAG2))
                        c = slice(HALF + h * HALF // 2, HALF + (h + 1) * HALF // 2)
                        act.activation(T[:, c], z[:, c], ACT.Sigmoid, scale=-1.0).then_inc(S["sig2"], 1)
                if first:
                    act.wait_ge(S["sig1"], s + 1)
                    act.activation(T[:, 0:HALF], T[:, 0:HALF], ACT.Ln, bias=tiny[:, 0:1]).then_inc(S["log_done"], 1)
                if second:
                    act.wait_ge(S["sig2"], 2 * (s - LAG2 + 1))
                    act.activation(T[:, HALF:], T[:, HALF:], ACT.Ln, bias=tiny[:, 0:1]).then_inc(S["log_done"], 1)
                for part in ([0] if first else []) + ([1] if second else []):
                    act.wait_ge(S["log_done"], logs(s, part))
                    for h in range(2):
                        c = slice(part * HALF + h * HALF // 2, part * HALF + (h + 1) * HALF // 2)
                        act.activation(T[:, c], T[:, c], ACT.Tanh, scale=-1.0).then_inc(S["tanh2" if part else "tanh1"], 1)
            for q in range(2 * KC):
                act.wait_ge(S["wt_done"], q + 1)
                act.activation((WsT if q < KC else WnT)[:, q % KC, :], bank[3 + q % 2][:, :], ACT.Copy).then_inc(S["wt_ready"], 1)
                if q == 3:
                    act.wait_ge(S["zu_ready"], 1)
                    act.activation(tu, zu, ACT.Sigmoid, scale=-1.0).then_inc(S["act_chain"], 1)
                    act.wait_ge(S["act_chain"], 1)
                    act.activation(tu, tu, ACT.Ln, bias=tiny[:, 0:1]).then_inc(S["act_chain"], 1)
                    act.wait_ge(S["act_chain"], 2)
                    act.activation(tu, tu, ACT.Tanh, scale=-1.0).then_inc(S["u_act"], 1)

        @block.tensor
        def _(pe):
            mm = nc.tensor.matmul

            def transpose4(dst, src, signal):
                for c in range(KC):
                    last = nc.tensor.transpose(quarter(dst, c), src[:, P * c:P * (c + 1)], ident[:, :])
                last.then_inc(signal, 1)

            def nodes_by(dst, lhs, rhs, signal, parts=KC):
                for c in range(parts):
                    last = mm(dst[:, :], lhs[:, c, :], rhs[:, c, :], start=c == 0, stop=c == parts - 1)
                last.then_inc(signal, 1)

            def features_by(dst, j0, js, w, rhs, parts, signal, c0=0):
                for j in js:
                    for c in range(parts):
                        last = mm(quarter(dst, j - j0), w[:, c0 + c, P * j:P * (j + 1)], rhs[:, c, :], start=c == 0, stop=c == parts - 1)
                last.then_inc(signal, 1)

            pe.wait_ge(S["ident_ready"], 1)
            pe.wait_ge(S["x_in"], 16)
            transpose4(bank[1], xs, S["x_transposed"])
            pe.wait_ge(S["vecs_in"], 16 * len(COLS))
            nc.tensor.transpose(bank[7][:, 0:24], vecs[:, :], ident[0:24, 0:24]).then_inc(S["cols_done"], 1)
            pe.wait_ge(S["xT_ready"], 1)
            pe.wait_ge(S["wq_in"], 16)
            features_by(bank[2], 0, range(KC), Wq, xT, KC, S["q_done"])
            pe.wait_ge(S["wk_in"], 16)
            features_by(bank[3], 0, range(KC), Wk, xT, KC, S["k_done"])
            pe.wait_ge(S["wv_in"], 16)
            nodes_by(bank[4], xT, Wv, S["v_done"])
            pe.wait_ge(S["onehot_bf"], 2)
            for t in range(ET):
                last = mm(bank[5][:, 0:N], Dbf[:, t, :], Sbf[:, t, :], start=t == 0, stop=t == ET - 1)
            last.then_inc(S["ct_done"], 1)
            pe.wait_ge(S["qk_ready"], 2 * KC)
            for h in range(HEADS):
                o, j = h % 2, h // 2
                part = slice(HEAD * o, HEAD * (o + 1))
                last = mm(quarter(bank[1] if o == 0 else bank[7], j), kT[part, j, :], qT[part, j, :], start=True, stop=True)
            last.then_inc(S["scores_done"], 1)
            pe.wait_ge(S["graphT_ready"], 2)
            nc.tensor.transpose(bank[6][:, 0:N], Ahat[:, :], ident[:, :])
            nc.tensor.transpose(bank[6][:, N:2 * N], Cn[:, :], ident[:, :]).then_inc(S["graphT_done"], 1)
            pe.wait_ge(S["attn_ready"], 1)
            pe.wait_ge(S["v_ready"], 1)
            for h in range(HEADS):
                o, j = h % 2, h // 2
                last = mm(bank[2][HEAD * o:HEAD * (o + 1), P * j:P * (j + 1)], v_sb[:, HEAD * h:HEAD * (h + 1)], attn[:, o, j, :], start=True, stop=True)
            last.then_inc(S["ao_done"], 1)
            pe.wait_ge(S["wo_in"], 16)
            pe.wait_ge(S["ao_ready"], 1)
            nodes_by(bank[3], aoT, Wo, S["wo_done"])
            pe.wait_ge(S["ea_split"], 1)
            pe.wait_ge(S["graph_ready"], 2)
            for q in range(ET // 4):
                if q >= 2:
                    pe.wait_ge(S["ea_Tready"], q - 1)
                for k in range(4):
                    last = nc.tensor.transpose(quarter(bank[5 + q % 2], k), EAs[:, 4 * q + k, :], ident[:, :])
                last.then_inc(S["ea_T"], 1)
            pe.wait_ge(S["nx_ready"], 1)
            transpose4(bank[1], y, S["nT_done"])
            pe.wait_ge(S["nT_ready"], 1)
            pe.wait_ge(S["f1_in"], 16)
            pe.wait_ge(S["ea_Tready"], ET // 4)
            for i, b in enumerate((bank[2], bank[4], bank[5], bank[6])):
                features_by(b, 2 * i, (2 * i, 2 * i + 1), F1, xT, KC, S["f1_done"])
            pe.wait_ge(S["f2_in"], 16)
            pe.wait_ge(S["ff_ready"], FC)
            nodes_by(bank[3], ffT, F2, S["f2_done"], FC)
            pe.wait_ge(S["nx_ready"], 3)
            transpose4(bank[1], xs, S["nT_done"])
            pe.wait_ge(S["nT_ready"], 2)
            pe.wait_ge(S["w1ab_in"], 16)
            nodes_by(bank[2], xT, W1ab[:, 0:KC, :], S["ab_done"])
            nodes_by(bank[4], xT, W1ab[:, KC:, :], S["ab_done"])
            pe.wait_ge(S["ab_ready"], 4)
            pe.wait_ge(S["c_split"], 1)
            pe.wait_ge(S["w2_split"], 1)
            for s in range(G + LAG3):
                if s < G:
                    edges = slice(GE * s, GE * (s + 1))
                    for j in range(KC):
                        u = KC * s + j
                        if u >= 2:
                            pe.wait_ge(S["z1_read"], u - 1)
                        f = slice(P * j, P * (j + 1))
                        terms = [(Ahi, ST), (Alo, ST), (Bhi, DT), (Blo, DT), (Chi, EAT), (Clo, EAT)]
                        for i, (w, x) in enumerate(terms):
                            last = mm(ST1[j % 2][:, :], w[:, f], x[:, edges], start=i == 0, stop=i == len(terms) - 1)
                        last.then_inc(S["z1_done"], 1)
                if s >= LAG3:
                    g = s - LAG3
                    pe.wait_ge(S["m_oh"], g + 1)
                    pe.wait_ge(S["m_lo"], g + 1)
                    for t in range(GT):
                        mm(AGG[:, :], Dg[:, t, :], Mhi[:, t, :], start=g == 0 and t == 0, stop=False)
                        last = mm(AGG[:, :], Dg[:, t, :], Mlo[:, t, :], start=False, stop=g == G - 1 and t == GT - 1)
                    last.then_inc(S["agg_done"], 1)
                if LAG2 <= s < G + LAG2:
                    g = s - LAG2
                    pe.wait_ge(S["h_lo"], g + 1)
                    hh, hl = Hhi[:, g % 2], Hlo[:, g % 2]
                    for t in range(GT):
                        if g >= 1:
                            pe.wait_ge(S["z2_read"], GT * (g - 1) + t + 1)
                        e = slice(P * t, P * (t + 1))
                        for c in range(KC):
                            for i, (h, w) in enumerate([(hh, W2hi), (hh, W2lo), (hl, W2hi)]):
                                last = mm(ST2[t][:, :], h[:, c, e], w[:, c, :], start=c == 0 and i == 0, stop=c == KC - 1 and i == 2)
                        last.then_inc(S["z2_done"], 1)
                if s == G + LAG2:
                    pe.wait_ge(S["w3_in"], 16)
                    features_by(bank[7], 0, range(KC), W3, xT, KC, S["ux_done"])
            pe.wait_ge(S["agg_ready"], 1)
            transpose4(bank[1], agg_sb, S["aggT_done"])
            pe.wait_ge(S["aggT_ready"], 1)
            features_by(bank[2], 0, range(KC), W3, aggT, KC, S["u_done"], c0=KC)

            def turn(q):
                w = WsR if q < KC else WnR
                if q >= 2:
                    pe.wait_ge(S["wt_ready"], q - 1)
                for k in range(KC):
                    last = nc.tensor.transpose(quarter(bank[3 + q % 2], k), w[:, k, P * (q % KC):P * (q % KC + 1)], ident[:, :])
                last.then_inc(S["wt_done"], 1)

            pe.wait_ge(S["ws_in"], 16)
            pe.wait_ge(S["wn_in"], 16)
            for q in range(4):
                turn(q)
            pe.wait_ge(S["u_ready"], 1)
            pe.wait_ge(S["w4_in"], 16)
            nodes_by(bank[5], uT, W4, S["o_done"])
            for q in range(4, 8):
                turn(q)
            pe.wait_ge(S["nx_ready"], 5)
            transpose4(bank[1], xs, S["nT_done"])
            pe.wait_ge(S["nT_ready"], 3)
            pe.wait_ge(S["g_in"], 32)
            for c in range(KC):
                last = mm(bank[2][:, 0:HID2], xT[:, c, :], G1[:, c, :], start=c == 0, stop=c == KC - 1)
            last.then_inc(S["g0_done"], 1)
            pe.wait_ge(S["wt_ready"], 2 * KC)
            pe.wait_ge(S["g0_ready"], 1)
            mm(bank[3][:, 0:HID2], Ahat[:, :], h0g, start=True, stop=True).then_inc(S["g1_done"], 1)
            pe.wait_ge(S["g1_ready"], 1)
            mm(bank[4][:, 0:N], r1g, Ahat[:, :], start=True, stop=True).then_inc(S["g2_done"], 1)
            pe.wait_ge(S["g2_ready"], 1)
            mm(bank[5][:, :], p1g, G2, start=True, stop=True).then_inc(S["g3_done"], 1)
            pe.wait_ge(S["nx_ready"], 6)
            transpose4(bank[1], xs, S["nT_done"])
            for j in range(KC):
                last = mm(quarter(bank[2], j), xs[:, P * j:P * (j + 1)], Cn[:, :], start=True, stop=True)
            last.then_inc(S["nm_done"], 1)
            pe.wait_ge(S["nT_ready"], 4)
            for c in range(KC):
                mm(bank[6][:, :], xT[:, c, :], WsT[:, c, :], start=c == 0, stop=False)
            pe.wait_ge(S["nm_ready"], 1)
            for c in range(KC):
                last = mm(bank[6][:, :], nmT[:, c, :], WnT[:, c, :], start=False, stop=c == KC - 1)
            last.then_inc(S["l3_done"], 1)

        @block.vector
        def _(dve):
            v = nc.vector
            chain = hop(dve, "dve_chain")
            norms = [0]

            def norm(src, dst):
                norms[0] += 1
                chain(v.bn_stats(stats[:, :], src))
                chain(v.bn_aggr(mv[:, :], stats[:, :]))
                v.tensor_scalar(mv[:, 1:2], mv[:, 1:2], EPS, None, ALU.add).then_inc(S["stat_ready"], 1)
                dve.wait_ge(S["rstd_ready"], norms[0])
                return v.tensor_scalar(dst, src, mv[:, 0:1], rstd[:, 0:1], ALU.subtract, ALU.mult)

            def r(name):
                return rows[:, slot[name], :]

            dve.wait_ge(S["consts"], 3)
            v.tensor_scalar(ident[:, :], iota_row[:, :], iota_col[:, 0:1], None, ALU.is_equal).then_inc(S["ident_ready"], 1)
            chain(v.memset(tiny[:, :], TINY))
            dve.wait_ge(S["ids_in"], 32)
            for ids, one in ((dcol, Dbf), (scol, Sbf)):
                if one is Sbf:
                    dve.wait_ge(S["x_transposed"], 1)
                    v.tensor_copy(xT[:, :, :].rearrange("p c n -> p (c n)"), bank[1][:, :]).then_inc(S["xT_ready"], 1)
                    dve.wait_ge(S["cols_done"], 1)
                    v.tensor_copy(cols[:, :], bank[7][:, 0:24]).then_inc(S["cols_ready"], 1)
                v.tensor_tensor(one, ids[:, :].unsqueeze(2).to_broadcast([P, ET, N]),
                                iota_row[:, :].unsqueeze(1).to_broadcast([P, ET, N]), ALU.is_equal).then_inc(S["onehot_bf"], 1)
            dve.wait_ge(S["v_done"], 1)
            dve.wait_ge(row_out, 2)
            v.tensor_tensor(v_sb, bank[4][:, :], r("L0_gnn_bv"), ALU.add).then_inc(S["v_ready"], 1)
            chain(v.tensor_tensor(xw[:, :], xs[:, :], r("L0_gnn_bo"), ALU.add))
            dve.wait_ge(S["ct_done"], 1)
            chain(v.tensor_copy(CTs[:, :], bank[5][:, 0:N]))
            chain(v.tensor_scalar(mask[:, :], CTs[:, :], 1.0, None, ALU.min))
            dve.wait_ge(S["scores_done"], 1)
            for o in range(2):
                v.tensor_tensor(attn[:, o], (bank[1] if o == 0 else bank[7])[:, :].rearrange("p (j n) -> p j n", j=KC),
                                mask[:, :].unsqueeze(1).to_broadcast([P, KC, N]), ALU.mult).then_inc(S["scores_read"], 1)
            dve.wait_ge(S["scores_read"], 2)
            flat = attn.rearrange("p o j n -> p (o j) n")
            by_node = attn.rearrange("p o j n -> p n (o j)")
            top = small_n[:, 0, :]
            chain(v.tensor_reduce(top, by_node, AX.X, ALU.max))
            v.tensor_tensor(flat, flat, top.unsqueeze(1).to_broadcast([P, HEADS, N]), ALU.subtract).then_inc(S["s_centred"], 1)
            chain(v.tensor_reduce(small[:, 0:1], CTs[:, :], AX.X, ALU.add))
            v.tensor_scalar(small[:, 1:2], small[:, 0:1], 1.0, None, ALU.add).then_inc(S["deg_ready"], 1)
            chain(v.tensor_scalar(small[:, 3:4], small[:, 0:1], 1.0, None, ALU.max))
            chain(v.reciprocal(small[:, 4:5], small[:, 3:4]))
            v.tensor_scalar(Cn[:, :], CTs[:, :], small[:, 4:5], None, ALU.mult).then_inc(S["graphT_ready"], 1)
            chain(v.tensor_tensor(mask[:, :], CTs[:, :], ident[:, :], ALU.add))
            dve.wait_ge(S["exp_done"], 1)
            total = small_n[:, 1, :]
            chain(v.tensor_reduce(total, by_node, AX.X, ALU.add))
            chain(v.reciprocal(total, total))
            v.tensor_tensor(flat, flat, total.unsqueeze(1).to_broadcast([P, HEADS, N]), ALU.mult).then_inc(S["attn_ready"], 1)
            for i, (ids, one) in enumerate(((src_bc, ST), (dst_bc, DT))):
                if i == 0:
                    dve.wait_ge(S["bc_ready"], 2)
                v.tensor_scalar(one[:, :].rearrange("n (t p) -> n t p", p=P), ids.rearrange("n (p t) -> n t p", p=P),
                                iota_col[:, 0:1], None, ALU.is_equal).then_inc(S["st_ready"], 1)
            dve.wait_ge(S["dinv_ready"], 1)
            v.tensor_scalar(Ahat[:, :], mask[:, :], small[:, 2:3], None, ALU.mult).then_inc(S["graphT_ready"], 1)
            dve.wait_ge(S["graphT_done"], 1)
            v.tensor_scalar(Ahat[:, :], bank[6][:, 0:N], small[:, 2:3], None, ALU.mult).then_inc(S["graph_ready"], 1)
            v.tensor_copy(Cn[:, :], bank[6][:, N:2 * N]).then_inc(S["graph_ready"], 1)
            dve.wait_ge(S["wc_in"], 32)
            chain(v.tensor_copy(Chi[:, :], Wc_raw[:, :]))
            v.tensor_tensor(Clo[:, :], Wc_raw[:, :], Chi[:, :].bitcast(F32), ALU.subtract).then_inc(S["c_split"], 1)
            dve.wait_ge(S["c_split"], 1)
            dve.wait_ge(S["wo_done"], 1)
            chain(v.tensor_tensor(y[:, :], bank[3][:, :], xw[:, :], ALU.add))
            chain(norm(y[:, :], y[:, :]))
            dve.wait_ge(row_out, 4)
            chain(v.tensor_tensor(y[:, :], y[:, :], r("L0_gnn_g1"), ALU.mult))
            v.tensor_tensor(y[:, :], y[:, :], r("L0_gnn_be1"), ALU.add).then_inc(S["nx_ready"], 1)
            dve.wait_ge(S["nT_done"], 1)
            v.tensor_copy(xT[:, :, :].rearrange("p c n -> p (c n)"), bank[1][:, :]).then_inc(S["nT_ready"], 1)
            dve.wait_ge(row_out, 7)
            dve.wait_ge(S["nx_ready"], 1)
            chain(v.tensor_tensor(xw[:, :], y[:, :], r("L0_gnn_b2"), ALU.add))
            dve.wait_ge(S["f2_done"], 1)
            chain(v.tensor_tensor(y[:, :], bank[3][:, :], xw[:, :], ALU.add))
            chain(norm(y[:, :], y[:, :]))
            chain(v.tensor_tensor(y[:, :], y[:, :], r("L0_gnn_g2"), ALU.mult))
            chain(v.tensor_tensor(xs[:, :], xs[:, :], r("L0_gnn_be2"), ALU.add))
            chain(v.tensor_tensor(y[:, :], y[:, :], xs[:, :], ALU.add))
            norm(y[:, :], xs[:, :]).then_inc(S["nx_ready"], 2)
            dve.wait_ge(S["nT_done"], 2)
            v.tensor_copy(xT[:, :, :].rearrange("p c n -> p (c n)"), bank[1][:, :]).then_inc(S["nT_ready"], 1)
            for i, (hi, lo, b) in enumerate(((Ahi, Alo, bank[2]), (Bhi, Blo, bank[4]))):
                dve.wait_ge(S["ab_done"], i + 1)
                v.tensor_copy(hi[:, :], b[:, :]).then_inc(S["ab_ready"], 1)
                dve.wait_ge(S["ab_ready"], 2 * i + 1)
                v.tensor_tensor(lo[:, :], b[:, :], hi[:, :].bitcast(F32), ALU.subtract).then_inc(S["ab_ready"], 1)
            dve.wait_ge(row_out, 8)

            def z1_out(s, j):
                dve.wait_ge(S["z1_done"], KC * s + j + 1)
                if j == 0 and s >= 2:
                    dve.wait_ge(S["h_lo"], s - 1)
                c = col["L1_gnn_b1"] + j
                v.tensor_scalar(Z[:, s % 2, GE * j:GE * (j + 1)], ST1[j % 2][:, :], cols[:, c:c + 1], None, ALU.add).then_inc(S["z1_read"], 1)

            def z2_out(s, t):
                g = s - LAG2
                dve.wait_ge(S["z2_done"], GT * g + t + 1)
                if t == 0 and g >= 2:
                    dve.wait_ge(S["m_lo"], g - 1)
                at = HALF + D * t
                v.tensor_tensor(Z[:, s % 2, at:at + D], ST2[t][:, :], r("L1_gnn_b2"), ALU.add).then_inc(S["z2_read"], 1)

            def product(b, part, h):
                n = 2 * (b - LAG2 if part else b) + h + 1
                dve.wait_ge(S["tanh2" if part else "tanh1"], n)
                c = slice(part * HALF + h * HALF // 2, part * HALF + (h + 1) * HALF // 2)
                z = Z[:, b % 2, c]
                v.tensor_tensor(z, z, T[:, c], ALU.mult).then_inc(S["m_mul" if part else "h_mul"], 1)

            def h_high(b):
                dve.wait_ge(S["h_mul"], 2 * (b + 1))
                if b >= 2:
                    dve.wait_ge(S["z2_done"], GT * (b - 1))
                v.tensor_copy(Hhi[:, b % 2, :, :].rearrange("p k n -> p (k n)"), Z[:, b % 2, 0:HALF]).then_inc(S["h_hi"], 1)

            def m_high(b):
                g = b - LAG2
                dve.wait_ge(S["m_mul"], 2 * (g + 1))
                if g >= 1:
                    dve.wait_ge(S["agg_done"], g)
                v.tensor_copy(Mhi[:, :, :].rearrange("p t n -> p (t n)"), Z[:, b % 2, HALF:]).then_inc(S["m_hi"], 1)
                v.tensor_tensor(Dg[:, :, :], dcol[:, GT * g:GT * (g + 1)].unsqueeze(2).to_broadcast([P, GT, N]),
                                iota_row[:, :].unsqueeze(1).to_broadcast([P, GT, N]), ALU.is_equal).then_inc(S["m_oh"], 1)

            for s in range(G + LAG2 + 1):
                b = s - 1
                first, second = 0 <= b < G, LAG2 <= b
                if s < G:
                    for j in range(KC):
                        z1_out(s, j)
                out2 = LAG2 <= s < G + LAG2
                if first:
                    product(b, 0, 0)
                if out2:
                    z2_out(s, 0)
                if first:
                    product(b, 0, 1)
                    h_high(b)
                if second:
                    product(b, 1, 0)
                if out2:
                    z2_out(s, 1)
                if second:
                    product(b, 1, 1)
                    m_high(b)
                if out2:
                    z2_out(s, 2)
                    z2_out(s, 3)
            dve.wait_ge(S["ux_done"], 1)
            c = col["L1_gnn_b3"]
            v.tensor_tensor(chunks(ux, KC), bank[7][:, :].rearrange("p (j n) -> p j n", j=KC),
                            cols[:, c:c + KC].unsqueeze(2).to_broadcast([P, KC, N]), ALU.add).then_inc(S["ux_ready"], 1)
            dve.wait_ge(row_out, 15)
            chain(v.tensor_tensor(xw[:, :], xs[:, :], r("L1_gnn_b4"), ALU.add))
            dve.wait_ge(S["agg_done"], G)
            v.tensor_copy(agg_sb, AGG[:, :]).then_inc(S["agg_ready"], 1)
            dve.wait_ge(S["aggT_done"], 1)
            v.tensor_copy(aggT.rearrange("p c n -> p (c n)"), bank[1][:, :]).then_inc(S["aggT_ready"], 1)
            dve.wait_ge(S["u_done"], 1)
            dve.wait_ge(S["ux_ready"], 1)
            v.tensor_tensor(zu, bank[2][:, :], ux, ALU.add).then_inc(S["zu_ready"], 1)
            dve.wait_ge(S["u_act"], 1)
            v.tensor_tensor(uT.rearrange("p c n -> p (c n)"), zu, tu, ALU.mult).then_inc(S["u_ready"], 1)
            dve.wait_ge(S["o_done"], 1)
            chain(v.tensor_tensor(y[:, :], bank[5][:, :], xw[:, :], ALU.add))
            chain(norm(y[:, :], y[:, :]))
            chain(v.tensor_tensor(y[:, :], y[:, :], r("L1_gnn_gamma"), ALU.mult))
            chain(v.tensor_tensor(xs[:, :], xs[:, :], r("L1_gnn_beta"), ALU.add))
            chain(v.tensor_tensor(y[:, :], y[:, :], xs[:, :], ALU.add))
            norm(y[:, :], xs[:, :]).then_inc(S["nx_ready"], 2)
            dve.wait_ge(S["nT_done"], 3)
            v.tensor_copy(xT[:, :, :].rearrange("p c n -> p (c n)"), bank[1][:, :]).then_inc(S["nT_ready"], 1)
            dve.wait_ge(S["nx_ready"], 5)
            chain(v.tensor_tensor(xw[:, :], xs[:, :], r("L2_gnn_b2"), ALU.add))
            dve.wait_ge(S["g0_done"], 1)
            v.tensor_copy(h0g, bank[2][:, 0:HID2]).then_inc(S["g0_ready"], 1)
            dve.wait_ge(S["g1_done"], 1)
            dve.wait_ge(S["b1g_in"], 16)
            chain(v.tensor_tensor(r1g, bank[3][:, 0:HID2], b1g[:, :], ALU.add))
            v.tensor_scalar(r1g, r1g, 0.0, None, ALU.max).then_inc(S["g1_ready"], 1)
            dve.wait_ge(S["g2_done"], 1)
            v.tensor_copy(p1g, bank[4][:, 0:N]).then_inc(S["g2_ready"], 1)
            dve.wait_ge(S["g3_done"], 1)
            chain(v.tensor_tensor(y[:, :], bank[5][:, :], xw[:, :], ALU.add))
            norm(y[:, :], xs[:, :]).then_inc(S["nx_ready"], 1)
            dve.wait_ge(S["nT_done"], 4)
            v.tensor_copy(xT[:, :, :].rearrange("p c n -> p (c n)"), bank[1][:, :]).then_inc(S["nT_ready"], 1)
            dve.wait_ge(S["nm_done"], 1)
            v.tensor_copy(nmT.rearrange("p c n -> p (c n)"), bank[2][:, :]).then_inc(S["nm_ready"], 1)
            dve.wait_ge(S["nx_ready"], 6)
            chain(v.tensor_tensor(xs[:, :], xs[:, :], r("L3_gnn_beta"), ALU.add))
            dve.wait_ge(S["l3_done"], 1)
            chain(v.tensor_tensor(y[:, :], bank[6][:, :], r("L3_gnn_bias"), ALU.add))
            chain(norm(y[:, :], y[:, :]))
            chain(v.tensor_tensor(y[:, :], y[:, :], r("L3_gnn_gamma"), ALU.mult))
            chain(v.tensor_tensor(y[:, :], y[:, :], xs[:, :], ALU.add))
            norm(y[:, :], y[:, :]).then_inc(S["y_final"], 1)


def kernel(**inputs):
    import numpy as np
    import concourse.bacc as bacc
    from concourse import mybir as mb
    from concourse.bass_utils import run_bass_kernel_spmd as run

    nc = bacc.Bacc("TRN2", target_bir_lowering=False, num_devices=1)
    arrays, args = {}, {}
    for name, value in inputs.items():
        v = np.ascontiguousarray(value)
        arrays[f"in_{name}"] = v
        args[name] = nc.dram_tensor(f"in_{name}", v.shape, mb.dt.from_np(v.dtype), kind="ExternalInput").ap()
    out = nc.dram_tensor("out_0", (N, D), F32, kind="ExternalOutput").ap()
    gnn_kernel(nc, args, out)
    r = run(nc, [arrays], core_ids=[0])
    return r.results[0]["out_0"]
```

```python
import concourse.bass as bass
from concourse import mybir
from contextlib import ExitStack

F32 = mybir.dt.float32
F32R = mybir.dt.float32r
BF16 = mybir.dt.bfloat16
I32 = mybir.dt.int32
ALU = mybir.AluOpType
ACT = mybir.ActivationFunctionType
AX = mybir.AxisListType

P = 128
N = 128
D = 512
KC = D // P
E = 4096
ET = E // P
EDIM = 64
HEADS = 8
HEAD = D // HEADS
FF = 2 * D
FC = FF // P
HID2 = 128
EPS = 1e-5
GT = 4
GE = GT * P
G = E // GE
LAG2 = 2
LAG3 = 4
HALF = KC * GE
TINY = 2.0 ** -63

ROWS = ["L0_gnn_bv", "L0_gnn_bo", "L0_gnn_g1", "L0_gnn_be1", "L0_gnn_b2", "L0_gnn_g2", "L0_gnn_be2",
        "L1_gnn_b2", "L1_gnn_b4", "L1_gnn_gamma", "L1_gnn_beta", "L2_gnn_b2",
        "L3_gnn_bias", "L3_gnn_gamma", "L3_gnn_beta"]
COLS = [("L0_gnn_bq", KC), ("L0_gnn_bk", KC), ("L0_gnn_b1", FC), ("L1_gnn_b1", KC), ("L1_gnn_b3", KC)]


def gnn_kernel(nc, a, out):
    ctx = ExitStack()
    with ctx:
        def sb(name, shape, dt=F32):
            return ctx.enter_context(nc.sbuf_tensor(name, shape, dt))

        def sem(name):
            return ctx.enter_context(nc.semaphore(name))

        Z = sb("Z", [P, 2, 2 * HALF])
        T = sb("T", [P, 2 * HALF])
        Dg = sb("Dg", [P, GT, N], F32R)
        Chi = sb("Chi", [P, D], F32R)
        Clo = sb("Clo", [P, D], F32R)
        rows = sb("rows", [P, 8, D])
        vecs = sb("vecs", [24, P])
        cols = sb("cols", [P, 24])
        b1g = sb("b1g", [P, HID2])
        xs = sb("xs", [P, D])
        xT = sb("xT", [P, KC, N])
        xw = sb("xw", [P, D])
        y = sb("y", [P, D])
        iota_row = sb("iota_row", [P, P])
        iota_col = sb("iota_col", [P, 1])
        ident = sb("ident", [P, P])
        dcol = sb("dcol", [P, ET], I32)
        scol = sb("scol", [P, ET], I32)
        Ahat = sb("Ahat", [P, N])
        Cn = sb("Cn", [P, N])
        CTs = sb("CTs", [P, N])
        mask = sb("mask", [P, N])
        small = sb("small", [P, 16])
        stats = sb("stats", [P, 6])
        mv = sb("mv", [P, 2])
        rstd = sb("rstd", [P, 1])
        mhalf = sb("mhalf", [P, 1])
        tiny = sb("tiny", [P, 1])
        small_n = sb("small_n", [P, 2, N])

        Z0, Z1 = Z[:, 0, :], Z[:, 1, :]

        def chunks(v, k):
            return v.rearrange("p (c n) -> p c n", c=k)

        def stage(*tensors):
            with ExitStack() as st:
                made = []
                for name, words, dt in tensors:
                    t = st.enter_context(nc.sbuf_tensor(name, [P, words], dt))
                    made.append(t[:, :])
            return [t for t, (name, _, _) in zip(made, tensors) if not name.startswith("pad")]

        W = KC * D
        Wq, Wk, Wv, Wo, MA, MB, Dbf, Sbf, ea_raw, rowvec8, idrow0 = stage(
            ("Wq", W, F32), ("Wk", W, F32), ("Wv", W, F32), ("Wo", W, F32), ("MA", W, F32), ("MB", W, F32),
            ("Dbf", 2 * W, BF16), ("Sbf", 2 * W, BF16), ("ea_raw", W, F32), ("pad0", E, F32), ("rowvec8", E, F32), ("idrow", E, I32))
        Hhi, Hlo, Mhi, Mlo, W2hi, W2lo, Ahi, Alo, Bhi, Blo, ST, DT, EAT = stage(
            ("Hhi", 2 * W, F32R),
            ("Hlo", 2 * W, F32R),
            ("Mhi", W, F32R), ("Mlo", W, F32R),
            ("W2hi", W, F32R), ("W2lo", W, F32R),
            ("Ahi", D, F32R), ("Alo", D, F32R), ("Bhi", D, F32R), ("Blo", D, F32R),
            ("ST", E, F32R), ("DT", E, F32R),
            ("EAT", E, F32R))
        WsT, WnT, tail, WsR, WnR, W4, G1, G2, W3 = stage(
            ("WsT", W, F32), ("WnT", W, F32), ("tail", 2 * W, F32), ("pad1", 5 * W, F32),
            ("WsR", W, F32), ("WnR", W, F32), ("W4", W, F32), ("G1", D, F32), ("G2", D, F32),
            ("pad2", 2 * D, F32), ("W3", 2 * W, F32))
        stage_bytes = ctx.enter_context(nc.sbuf_tensor("stages", [P, 15 * W], F32))

        Wq, Wk, Wv, Wo, W4, WsR, WnR, WsT, WnT, G1 = (chunks(w, KC) for w in (Wq, Wk, Wv, Wo, W4, WsR, WnR, WsT, WnT, G1))
        W2hi, W2lo = chunks(W2hi, KC), chunks(W2lo, KC)
        W3 = chunks(W3, 2 * KC)
        Hhi, Hlo = (h.rearrange("p (a k n) -> p a k n", a=2, k=KC) for h in (Hhi, Hlo))
        Mhi, Mlo = chunks(Mhi, GT), chunks(Mlo, GT)
        Dbf, Sbf = chunks(Dbf, ET), chunks(Sbf, ET)
        W2raw = chunks(ea_raw, KC)
        ea_raw = chunks(ea_raw, ET)
        F1 = chunks(T[:, :], KC)
        F2 = chunks(Z0, FC)
        src_bc, dst_bc = Z0.bitcast(I32), Z1.bitcast(I32)
        EAs = chunks(Z0, ET)
        W1ab = chunks(Z1, 2 * KC)
        qT = chunks(MA[:, 0:D], KC)
        kT = chunks(MA[:, D:2 * D], KC)
        v_sb = MA[:, 2 * D:3 * D]
        aoT = chunks(MA[:, 3 * D:4 * D], KC)
        attn = MB[:, 0:2 * D].rearrange("p (o j n) -> p o j n", o=2, j=KC)
        ffT = chunks(MB[:, 2 * D:4 * D], FC)
        xb = MA[:, D:2 * D]
        xb_late = tail[:, 7 * D:8 * D]
        Wc_raw = y
        idrow = [idrow0[0:1, :], T[0:1, :].bitcast(I32)]
        rowvec8 = chunks(rowvec8[0:1, :], 8)
        rowvec = sb("rowvec", [1, 2, D])
        ux = tail[:, 0:D]
        zu = tail[:, D:2 * D]
        tu = tail[:, 2 * D:3 * D]
        uT = chunks(tail[:, 3 * D:4 * D], KC)
        aggT = chunks(tail[:, 4 * D:5 * D], KC)
        agg_sb = tail[:, 5 * D:6 * D]
        r1g = tail[:, 6 * D + HID2:6 * D + 2 * HID2]
        p1g = tail[:, 6 * D + 2 * HID2:6 * D + 3 * HID2]
        nmT = chunks(tail[:, 7 * D:8 * D], KC)

        bank = [ctx.enter_context(nc.psum_tensor(f"bank{i}", [P, D], F32)) for i in range(8)]
        AGG, ST1, ST2 = bank[0], [bank[1], bank[2], bank[7]], bank[3:7]

        def quarter(b, j):
            return b[:, P * j:P * (j + 1)]

        col = {}
        at = 0
        for name, k in COLS:
            col[name] = at
            at += k
        slot = {name: i for i, name in enumerate(ROWS[:8])}
        again = ROWS[8:]
        slot.update({name: i for i, name in enumerate(again)})

        S = {}
        for name in ("x_in ids_in vecs_in ea_in wq_in wk_in wv_in wo_in f1_in f2_in w1ab_in wc_in w2_in w3_in w4_in g_in ws_in wn_in b1g_in "
                     "out_stored consts ident_ready x_transposed xT_ready cols_done cols_ready q_done k_done v_done "
                     "qk_ready v_ready onehot_bf ct_done ct_read scores_done scores_read s_centred exp_done attn_ready ao_done ao_ready wo_done "
                     "stat_ready rstd_ready nx_ready nT_done nT_ready f1_done ff_ready f2_done "
                     "ids_row bc_ready st_ready ea_hi ea_split ea_T ea_Tready w2_hi w2_split c_split ab_done ab_ready "
                     "graphT_ready graphT_done graph_ready deg_ready dinv_ready "
                     "z1_done z1_read z2_done z2_read sig1 sig2 log1 log2 tanh1 tanh2 h_mul h_hi h_lo m_mul m_hi m_lo m_lo_last m_oh agg_done st1_all "
                     "ux_done ux_ready agg_ready aggT_done aggT_ready u_done zu_ready u_act u_ready o_done "
                     "g0_done g0_ready g1_done g1_ready g2_done g2_ready g3_done nm_done nm_ready l3_done wt_done wt_ready y_final "
                     "dve_chain act_chain pool_chain").split():
            S[name] = sem(name)
        row_in = [sem(f"row_in{i}") for i in range(10)]
        row_out = sem("row_out")

        block = ctx.enter_context(nc.Block())

        def w_view(w):
            return w.rearrange("(c p) n -> p c n", p=P)

        def hop(eng, name):
            n = [0]

            def link(ins):
                n[0] += 1
                ins.then_inc(S[name], 1)
                eng.wait_ge(S[name], n[0])
            return link

        def z1(g):
            return chunks(Z[:, g % 2, 0:HALF], KC)

        def z2(g):
            return chunks(Z[:, g % 2, HALF:], GT)

        def units(g, j=0):
            return KC * g + j + (KC if g else 0)

        T1, T2 = chunks(T[:, 0:HALF], KC), chunks(T[:, HALF:], GT)

        @block.sync
        def _(sp):
            sp.dma_start(xs[:, :], a["x"]).then_inc(S["x_in"], 16)
            sp.dma_start(dcol[:, :], a["dst"].rearrange("(p t) -> p t", p=P)).then_inc(S["ids_in"], 16)
            sp.dma_start(Wq, w_view(a["L0_gnn_Wq"])).then_inc(S["wq_in"], 16)
            sp.wait_ge(S["vecs_in"], 16 * len(COLS))
            sp.dma_start(Wk, w_view(a["L0_gnn_Wk"])).then_inc(S["wk_in"], 16)
            sp.dma_start(ea_raw, a["edge_attr_64"].rearrange("(p t) n -> p t n", p=P)).then_inc(S["ea_in"], 16)
            sp.dma_start(Wv, w_view(a["L0_gnn_Wv"])).then_inc(S["wv_in"], 16)
            sp.dma_start(Wo, w_view(a["L0_gnn_Wo"])).then_inc(S["wo_in"], 16)
            sp.wait_ge(S["bc_ready"], 2)
            sp.dma_start(F1, w_view(a["L0_gnn_W1"])).then_inc(S["f1_in"], 16)
            sp.wait_ge(S["st_ready"], 2)
            sp.dma_start(W1ab, w_view(a["L1_gnn_W1"][0:2 * D, :])).then_inc(S["w1ab_in"], 16)
            sp.wait_ge(S["ea_split"], 1)
            sp.dma_start(W2raw, w_view(a["L1_gnn_W2"])).then_inc(S["w2_in"], 16)
            sp.wait_ge(S["ea_T"], 8)
            sp.dma_start(F2, w_view(a["L0_gnn_W2"])).then_inc(S["f2_in"], 16)
            for i in range(8, 15):
                if i >= 10:
                    sp.wait_ge(row_out, i - 1)
                sp.dma_start(rowvec[0:1, i % 2, :], a[ROWS[i]].rearrange("(o n) -> o n", o=1)).then_inc(row_in[8 + i % 2], 16)
            sp.wait_ge(S["z1_done"], units(G))
            sp.dma_start(W3, w_view(a["L1_gnn_W3"])).then_inc(S["w3_in"], 16)
            sp.dma_start(W4, w_view(a["L1_gnn_W4"])).then_inc(S["w4_in"], 16)
            sp.dma_start(G1, w_view(a["L2_gnn_W1"])).then_inc(S["g_in"], 16)
            sp.dma_start(G2, a["L2_gnn_W2"]).then_inc(S["g_in"], 16)
            sp.dma_start(WsR, w_view(a["L3_gnn_W_self"])).then_inc(S["ws_in"], 16)
            sp.dma_start(WnR, w_view(a["L3_gnn_W_neigh"])).then_inc(S["wn_in"], 16)
            sp.wait_ge(S["y_final"], 1)
            sp.dma_start(out, y[:, :]).then_inc(S["out_stored"], 16)
            sp.wait_ge(S["out_stored"], 16)

        @block.gpsimd
        def _(pool):
            chain = hop(pool, "pool_chain")
            pool.iota(iota_row[:, :], pattern=[[1, P]], base=0, channel_multiplier=0,
                      allow_small_or_imprecise_dtypes=True).then_inc(S["consts"], 1)
            pool.iota(iota_col[:, :], pattern=[[0, 1]], base=0, channel_multiplier=1,
                      allow_small_or_imprecise_dtypes=True).then_inc(S["consts"], 1)
            pool.memset(mhalf[:, :], -0.5).then_inc(S["consts"], 1)
            pool.wait_ge(S["consts"], 3)

            def row(i):
                if i < 8:
                    pool.wait_ge(row_in[i], 16)
                    src = rowvec8[:, i, :]
                else:
                    pool.wait_ge(row_in[8 + i % 2], 16 * (i // 2 - 3))
                    src = rowvec[0:1, i % 2, :]
                pool.partition_broadcast(rows[:, slot[ROWS[i]], :], src).then_inc(row_out, 1)

            def inverse_root(k, src, dst, ready, signal):
                pool.wait_ge(ready, k)
                pool.tensor_tensor(dst, src, mhalf[:, :], ALU.pow).then_inc(signal, 1)

            norms = [0]

            def norm():
                norms[0] += 1
                inverse_root(norms[0], mv[:, 1:2], rstd[:, :], S["stat_ready"], S["rstd_ready"])

            pool.wait_ge(S["ids_row"], 32)
            pool.partition_broadcast(src_bc, idrow[0]).then_inc(S["bc_ready"], 1)
            pool.partition_broadcast(dst_bc, idrow[1]).then_inc(S["bc_ready"], 1)
            row(0)
            pool.wait_ge(S["ea_hi"], 1)
            pool.tensor_tensor(EAs[:, :, EDIM:], ea_raw, EAs[:, :, 0:EDIM], ALU.subtract).then_inc(S["ea_split"], 1)
            for i in range(1, 8):
                row(i)
            inverse_root(1, small[:, 1:2], small[:, 2:3], S["deg_ready"], S["dinv_ready"])
            norm()
            pool.wait_ge(S["w2_hi"], 1)
            pool.tensor_tensor(W2lo[:, :, :], W2raw, W2hi.bitcast(F32), ALU.subtract).then_inc(S["w2_split"], 1)
            norm()
            norm()
            pool.wait_ge(S["nx_ready"], 3)
            for i in range(8, 15):
                row(i)
            def low(dst, z, high, signal):
                pool.tensor_tensor(dst, z, high.bitcast(F32), ALU.subtract).then_inc(signal, 1)

            for s in range(G + LAG2):
                if 1 <= s < G:
                    for h in range(2):
                        pool.wait_ge(S["h_hi"], 2 * s + h + 1)
                        e = slice(GE // 2 * h, GE // 2 * (h + 1))
                        low(Hlo[:, s % 2, :, e], z1(s)[:, :, e], Hhi[:, s % 2, :, e], S["h_lo"])
                if s >= LAG2:
                    g = s - LAG2
                    for h in range(1 if g == G - 1 else 2):
                        pool.wait_ge(S["m_hi"], 2 * g + h + 1)
                        t = slice(GT // 2 * h, GT // 2 * (h + 1))
                        low(Mlo[:, t, :], z2(g)[:, t, :], Mhi[:, t, :], S["m_lo"])
            for _ in range(5):
                norm()

        @block.scalar
        def _(act):
            act.dma_start(scol[:, :], a["src"].rearrange("(p t) -> p t", p=P)).then_inc(S["ids_in"], 16)
            act.dma_start(idrow[1], a["dst"].rearrange("(o n) -> o n", o=1)).then_inc(S["ids_row"], 16)
            act.dma_start(idrow[0], a["src"].rearrange("(o n) -> o n", o=1)).then_inc(S["ids_row"], 16)
            for name, k in COLS:
                act.dma_start(vecs[col[name]:col[name] + k, :], a[name].rearrange("(k p) -> k p", p=P)).then_inc(S["vecs_in"], 16)
            for i in range(8):
                act.dma_start(rowvec8[:, i, :], a[ROWS[i]].rearrange("(o n) -> o n", o=1)).then_inc(row_in[i], 16)
            for h in range(2):
                act.dma_start(Wc_raw[EDIM * h:EDIM * (h + 1), :], a["L1_gnn_W1"][2 * D:, :]).then_inc(S["wc_in"], 16)
            act.dma_start(b1g[:, :], a["L2_gnn_b1"].rearrange("(o n) -> o n", o=1).to_broadcast([P, HID2])).then_inc(S["b1g_in"], 16)

            def bias_out(dst, src, name, j, func=ACT.Identity):
                return act.activation(dst, src, func, bias=cols[:, col[name] + j:col[name] + j + 1])

            act.wait_ge(S["cols_done"], 1)
            act.activation(cols[:, :], bank[7][:, 0:24], ACT.Copy).then_inc(S["cols_ready"], 1)
            act.wait_ge(S["cols_ready"], 1)
            act.wait_ge(S["q_done"], 1)
            for j in range(KC):
                bias_out(qT[:, j, :], quarter(bank[2], j), "L0_gnn_bq", j).then_inc(S["qk_ready"], 1)
            act.wait_ge(S["k_done"], 1)
            for j in range(KC):
                bias_out(kT[:, j, :], quarter(bank[3], j), "L0_gnn_bk", j).then_inc(S["qk_ready"], 1)
            act.wait_ge(S["ea_in"], 16)
            act.wait_ge(S["st_ready"], 1)
            act.activation(EAs[:, :, 0:EDIM].bitcast(F32R), ea_raw, ACT.Copy).then_inc(S["ea_hi"], 1)
            act.wait_ge(S["s_centred"], 1)
            act.activation(attn.rearrange("p o j n -> p (o j n)"), attn.rearrange("p o j n -> p (o j n)"), ACT.Exp,
                           scale=float(HEAD) ** -0.5).then_inc(S["exp_done"], 1)
            for q in range(ET // 4):
                act.wait_ge(S["ea_T"], q + 1)
                act.activation(EAT[:, 4 * P * q:4 * P * (q + 1)], bank[5 + q % 2][:, :], ACT.Copy).then_inc(S["ea_Tready"], 1)
            for i in range(4):
                act.wait_ge(S["f1_done"], i + 1)
                for j in (2 * i, 2 * i + 1):
                    bias_out(ffT[:, j, :], quarter((bank[2], bank[4], bank[5], bank[6])[i], j % 2), "L0_gnn_b1", j,
                             ACT.Relu).then_inc(S["ff_ready"], 1)
            act.wait_ge(S["w2_in"], 16)
            act.activation(W2hi[:, :, :], W2raw, ACT.Copy).then_inc(S["w2_hi"], 1)
            def mish(g1, g2):
                t2 = T1 if g2 == G - 1 else T2
                if g1 is not None:
                    act.wait_ge(S["z1_read"], units(g1 + 1))
                    if g1 >= 1:
                        act.wait_ge(S["h_mul"], 2 * g1)
                    act.activation(T1, z1(g1), ACT.Sigmoid, scale=-1.0).then_inc(S["sig1"], 1)
                if g2 is not None:
                    for h in range(2):
                        act.wait_ge(S["z2_read"], GT * g2 + 2 * (h + 1))
                        if g2 == G - 1:
                            act.wait_ge(S["h_mul"], 2 * G)
                        elif g2 >= 1:
                            act.wait_ge(S["m_mul"], 2 * g2)
                        t = slice(2 * h, 2 * (h + 1))
                        act.activation(t2[:, t, :], z2(g2)[:, t, :], ACT.Sigmoid, scale=-1.0).then_inc(S["sig2"], 1)
                if g1 is not None:
                    act.wait_ge(S["sig1"], g1 + 2)
                    act.activation(T1, T1, ACT.Ln, bias=tiny[:, 0:1]).then_inc(S["log1"], 1)
                if g2 is not None:
                    act.wait_ge(S["sig2"], 2 * (g2 + 1))
                    act.activation(t2, t2, ACT.Ln, bias=tiny[:, 0:1]).then_inc(S["log2"], 1)
                act.preload_act_table_set("sigmoid_and_others")
                if g1 is not None:
                    act.wait_ge(S["log1"], g1 + 2)
                    for h in range(2):
                        e = slice(GE // 2 * h, GE // 2 * (h + 1))
                        act.activation(T1[:, :, e], T1[:, :, e], ACT.Tanh, scale=-1.0).then_inc(S["tanh1"], 1)
                if g2 is not None:
                    act.wait_ge(S["log2"], g2 + 1)
                    for h in range(2):
                        t = slice(2 * h, 2 * (h + 1))
                        act.activation(t2[:, t, :], t2[:, t, :], ACT.Tanh, scale=-1.0).then_inc(S["tanh2"], 1)

            for h in range(2):
                e = slice(GE // 2 * h, GE // 2 * (h + 1))
                act.wait_ge(S["z1_read"], KC * (h + 1))
                act.activation(T1[:, :, e], z1(0)[:, :, e], ACT.Sigmoid, scale=-1.0).then_inc(S["sig1"], 1)
                act.wait_ge(S["sig1"], h + 1)
                act.activation(T1[:, :, e], T1[:, :, e], ACT.Ln, bias=tiny[:, 0:1]).then_inc(S["log1"], 1)
                act.preload_act_table_set("sigmoid_and_others")
                act.wait_ge(S["log1"], h + 1)
                act.activation(T1[:, :, e], T1[:, :, e], ACT.Tanh, scale=-1.0).then_inc(S["tanh1"], 1)
            for g in range(1, G - 1):
                mish(g, g - LAG2 if g >= LAG2 else None)
            mish(G - 1, None)
            for g in range(G - 1 - LAG2, G):
                mish(None, g)
            act.wait_ge(S["zu_ready"], 1)
            act.activation(tu, zu, ACT.Sigmoid, scale=-1.0).then_inc(S["act_chain"], 1)
            act.wait_ge(S["act_chain"], 1)
            act.activation(tu, tu, ACT.Ln, bias=tiny[:, 0:1]).then_inc(S["act_chain"], 1)
            act.wait_ge(S["act_chain"], 2)
            act.activation(tu, tu, ACT.Tanh, scale=-1.0).then_inc(S["u_act"], 1)

        @block.tensor
        def _(pe):
            mm = nc.tensor.matmul

            def transpose4(dst, src, signal):
                for c in range(KC):
                    last = nc.tensor.transpose(quarter(dst, c), src[:, P * c:P * (c + 1)], ident[:, :])
                last.then_inc(signal, 1)

            def nodes_by(dst, lhs, rhs, signal, parts=KC):
                for c in range(parts):
                    last = mm(dst[:, :], lhs[:, c, :], rhs[:, c, :], start=c == 0, stop=c == parts - 1)
                last.then_inc(signal, 1)

            def features_by(dst, j0, js, w, rhs, parts, signal, c0=0):
                for j in js:
                    for c in range(parts):
                        last = mm(quarter(dst, j - j0), w[:, c0 + c, P * j:P * (j + 1)], rhs[:, c, :], start=c == 0, stop=c == parts - 1)
                last.then_inc(signal, 1)

            pe.wait_ge(S["ident_ready"], 1)
            pe.wait_ge(S["x_in"], 16)
            transpose4(bank[1], xs, S["x_transposed"])
            pe.wait_ge(S["vecs_in"], 16 * len(COLS))
            nc.tensor.transpose(bank[7][:, 0:24], vecs[:, :], ident[0:24, 0:24]).then_inc(S["cols_done"], 1)
            pe.wait_ge(S["xT_ready"], 1)
            pe.wait_ge(S["wq_in"], 16)
            features_by(bank[2], 0, range(KC), Wq, xT, KC, S["q_done"])
            pe.wait_ge(S["wk_in"], 16)
            features_by(bank[3], 0, range(KC), Wk, xT, KC, S["k_done"])
            pe.wait_ge(S["onehot_bf"], 2)
            for t in range(ET):
                last = mm(bank[5][:, 0:N], Dbf[:, t, :], Sbf[:, t, :], start=t == 0, stop=t == ET - 1)
            last.then_inc(S["ct_done"], 1)
            pe.wait_ge(S["qk_ready"], 2 * KC)
            for h in range(HEADS):
                o, j = h % 2, h // 2
                part = slice(HEAD * o, HEAD * (o + 1))
                last = mm(quarter(bank[1] if o == 0 else bank[7], j), kT[part, j, :], qT[part, j, :], start=True, stop=True)
            last.then_inc(S["scores_done"], 1)
            pe.wait_ge(S["wv_in"], 16)
            nodes_by(bank[4], xT, Wv, S["v_done"])
            def edge_transposes(lo, hi):
                for q in range(lo, hi):
                    if q >= 2:
                        pe.wait_ge(S["ea_Tready"], q - 1)
                    for k in range(4):
                        last = nc.tensor.transpose(quarter(bank[5 + q % 2], k), EAs[:, 4 * q + k, :], ident[:, :])
                    last.then_inc(S["ea_T"], 1)

            pe.wait_ge(S["ct_read"], 1)
            pe.wait_ge(S["ea_split"], 1)
            edge_transposes(0, 3)
            pe.wait_ge(S["attn_ready"], 1)
            pe.wait_ge(S["v_ready"], 1)
            for h in range(HEADS):
                o, j = h % 2, h // 2
                last = mm(bank[2][HEAD * o:HEAD * (o + 1), P * j:P * (j + 1)], v_sb[:, HEAD * h:HEAD * (h + 1)], attn[:, o, j, :], start=True, stop=True)
            last.then_inc(S["ao_done"], 1)
            pe.wait_ge(S["wo_in"], 16)
            pe.wait_ge(S["ao_ready"], 1)
            nodes_by(bank[3], aoT, Wo, S["wo_done"])
            edge_transposes(3, ET // 4)
            pe.wait_ge(S["graphT_ready"], 2)
            nc.tensor.transpose(bank[7][:, 0:N], Ahat[:, :], ident[:, :])
            nc.tensor.transpose(bank[7][:, N:2 * N], Cn[:, :], ident[:, :]).then_inc(S["graphT_done"], 1)
            pe.wait_ge(S["nx_ready"], 1)
            transpose4(bank[1], y, S["nT_done"])
            pe.wait_ge(S["nT_ready"], 1)
            pe.wait_ge(S["f1_in"], 16)
            pe.wait_ge(S["ea_Tready"], ET // 4)
            for i, b in enumerate((bank[2], bank[4], bank[5], bank[6])):
                features_by(b, 2 * i, (2 * i, 2 * i + 1), F1, xT, KC, S["f1_done"])
            pe.wait_ge(S["f2_in"], 16)
            pe.wait_ge(S["ff_ready"], FC)
            nodes_by(bank[3], ffT, F2, S["f2_done"], FC)
            pe.wait_ge(S["nx_ready"], 3)
            transpose4(bank[1], xs, S["nT_done"])
            pe.wait_ge(S["nT_ready"], 2)
            pe.wait_ge(S["w1ab_in"], 16)
            nodes_by(bank[2], xT, W1ab[:, 0:KC, :], S["ab_done"])
            nodes_by(bank[4], xT, W1ab[:, KC:, :], S["ab_done"])
            pe.wait_ge(S["ab_ready"], 2)
            pe.wait_ge(S["c_split"], 1)
            pe.wait_ge(S["w2_split"], 1)
            def first_layer(g):
                halves = 2 if g == 0 else 1
                width = GE // halves
                for i in range(halves * KC):
                    half, j = i // KC, i % KC
                    edges = slice(GE * g + width * half, GE * g + width * (half + 1))
                    u = units(g) + i
                    if u >= 3:
                        pe.wait_ge(S["z1_read"], u - 2)
                    f = slice(P * j, P * (j + 1))
                    terms = [(Chi, EAT), (Clo, EAT), (Ahi, ST), (Alo, ST), (Bhi, DT), (Blo, DT)]
                    for k, (w, x) in enumerate(terms):
                        if u == 0 and w is Bhi:
                            pe.wait_ge(S["ab_ready"], 4)
                        last = mm(ST1[u % 3][:, 0:width], w[:, f], x[:, edges], start=k == 0, stop=k == len(terms) - 1)
                    last.then_inc(S["z1_done"], 1)

            def second_layer(g, h):
                pe.wait_ge(S["h_lo"], 2 * g + h + 1)
                hh, hl = Hhi[:, g % 2], Hlo[:, g % 2]
                for t in (2 * h, 2 * h + 1):
                    if g >= 1:
                        pe.wait_ge(S["z2_read"], GT * (g - 1) + t + 1)
                    e = slice(P * t, P * (t + 1))
                    for c in range(KC):
                        for i, (x, w) in enumerate([(hh, W2hi), (hh, W2lo), (hl, W2hi)]):
                            last = mm(ST2[t][:, :], x[:, c, e], w[:, c, :], start=c == 0 and i == 0, stop=c == KC - 1 and i == 2)
                    last.then_inc(S["z2_done"], 1)

            def sum_messages(g):
                pe.wait_ge(S["m_oh"], g + 1)
                for t in range(GT):
                    pe.wait_ge(S["m_lo"], 2 * g + (1 if t < GT // 2 or g == G - 1 else 2))
                    if g == G - 1 and t == GT // 2:
                        pe.wait_ge(S["m_lo_last"], 1)
                    mm(AGG[:, :], Dg[:, t, :], Mhi[:, t, :], start=g == 0 and t == 0, stop=False)
                    last = mm(AGG[:, :], Dg[:, t, :], Mlo[:, t, :], start=False, stop=g == G - 1 and t == GT - 1)
                last.then_inc(S["agg_done"], 1)

            def turn(q):
                w = WsR if q < KC else WnR
                if q >= 2:
                    pe.wait_ge(S["wt_ready"], q - 1)
                for k in range(KC):
                    last = nc.tensor.transpose(quarter(bank[3 + q % 2], k), w[:, k, P * (q % KC):P * (q % KC + 1)], ident[:, :])
                last.then_inc(S["wt_done"], 1)

            for s in range(G + LAG2):
                if s < G:
                    first_layer(s)
                if s >= LAG2:
                    second_layer(s - LAG2, 0)
                    if LAG3 <= s <= G:
                        sum_messages(s - LAG3)
                    second_layer(s - LAG2, 1)
            sum_messages(G - 3)
            pe.wait_ge(S["w3_in"], 16)
            pe.wait_ge(S["z1_read"], units(G))
            features_by(bank[7], 0, range(KC), W3, xT, KC, S["ux_done"])
            sum_messages(G - 2)
            pe.wait_ge(S["ws_in"], 16)
            pe.wait_ge(S["wn_in"], 16)
            pe.wait_ge(S["z2_read"], GT * G)
            for q in range(2 * KC):
                turn(q)
            sum_messages(G - 1)
            pe.wait_ge(S["agg_ready"], 1)
            transpose4(bank[1], agg_sb, S["aggT_done"])
            pe.wait_ge(S["aggT_ready"], 1)
            features_by(bank[2], 0, range(KC), W3, aggT, KC, S["u_done"], c0=KC)

            pe.wait_ge(S["u_ready"], 1)
            pe.wait_ge(S["w4_in"], 16)
            nodes_by(bank[5], uT, W4, S["o_done"])
            pe.wait_ge(S["nx_ready"], 5)
            for j in range(KC):
                last = mm(quarter(bank[1], j), xs[:, P * j:P * (j + 1)], Ahat[:, :], start=True, stop=True)
            last.then_inc(S["g0_done"], 1)
            pe.wait_ge(S["g0_ready"], 1)
            pe.wait_ge(S["g_in"], 32)
            for c in range(KC):
                last = mm(bank[3][:, 0:HID2], xT[:, c, :], G1[:, c, :], start=c == 0, stop=c == KC - 1)
            last.then_inc(S["g1_done"], 1)
            pe.wait_ge(S["g1_ready"], 1)
            mm(bank[4][:, 0:N], r1g, Ahat[:, :], start=True, stop=True).then_inc(S["g2_done"], 1)
            pe.wait_ge(S["g2_ready"], 1)
            mm(bank[5][:, :], p1g, G2, start=True, stop=True).then_inc(S["g3_done"], 1)
            pe.wait_ge(S["nx_ready"], 6)
            transpose4(bank[1], xs, S["nT_done"])
            for j in range(KC):
                last = mm(quarter(bank[2], j), xs[:, P * j:P * (j + 1)], Cn[:, :], start=True, stop=True)
            last.then_inc(S["nm_done"], 1)
            pe.wait_ge(S["nT_ready"], 3)
            for c in range(KC):
                mm(bank[6][:, :], xT[:, c, :], WsT[:, c, :], start=c == 0, stop=False)
            pe.wait_ge(S["nm_ready"], 1)
            for c in range(KC):
                last = mm(bank[6][:, :], nmT[:, c, :], WnT[:, c, :], start=False, stop=c == KC - 1)
            last.then_inc(S["l3_done"], 1)

        @block.vector
        def _(dve):
            v = nc.vector
            chain = hop(dve, "dve_chain")
            norms = [0]

            def norm(src, dst):
                norms[0] += 1
                chain(v.bn_stats(stats[:, :], src))
                chain(v.bn_aggr(mv[:, :], stats[:, :]))
                v.tensor_scalar(mv[:, 1:2], mv[:, 1:2], EPS, None, ALU.add).then_inc(S["stat_ready"], 1)
                dve.wait_ge(S["rstd_ready"], norms[0])
                return v.tensor_scalar(dst, src, mv[:, 0:1], rstd[:, 0:1], ALU.subtract, ALU.mult)

            def norm_gain(src, dst, gain, plus):
                norms[0] += 1
                chain(v.bn_stats(stats[:, :], src))
                chain(v.bn_aggr(mv[:, :], stats[:, :]))
                v.tensor_scalar(mv[:, 1:2], mv[:, 1:2], EPS, None, ALU.add).then_inc(S["stat_ready"], 1)
                chain(v.scalar_tensor_tensor(out=src, in0=src, scalar=mv[:, 0:1], in1=gain, op0=ALU.subtract, op1=ALU.mult))
                dve.wait_ge(S["rstd_ready"], norms[0])
                return v.scalar_tensor_tensor(out=dst, in0=src, scalar=rstd[:, 0:1], in1=plus, op0=ALU.mult, op1=ALU.add)

            def r(name):
                return rows[:, slot[name], :]

            dve.wait_ge(S["consts"], 3)
            v.tensor_scalar(ident[:, :], iota_row[:, :], iota_col[:, 0:1], None, ALU.is_equal).then_inc(S["ident_ready"], 1)
            chain(v.memset(tiny[:, :], TINY))
            dve.wait_ge(S["x_transposed"], 1)
            v.tensor_copy(xT[:, :, :].rearrange("p c n -> p (c n)"), bank[1][:, :]).then_inc(S["xT_ready"], 1)
            dve.wait_ge(S["ids_in"], 32)
            for ids, one in ((dcol, Dbf), (scol, Sbf)):
                v.tensor_tensor(one, ids[:, :].unsqueeze(2).to_broadcast([P, ET, N]),
                                iota_row[:, :].unsqueeze(1).to_broadcast([P, ET, N]), ALU.is_equal).then_inc(S["onehot_bf"], 1)
            def node_hot(one, ids):
                v.tensor_scalar(one[:, :].rearrange("n (t p) -> n t p", p=P), ids.rearrange("n (p t) -> n t p", p=P),
                                iota_col[:, 0:1], None, ALU.is_equal).then_inc(S["st_ready"], 1)

            dve.wait_ge(S["bc_ready"], 1)
            node_hot(ST, src_bc)
            dve.wait_ge(S["ct_done"], 1)
            v.tensor_copy(CTs[:, :], bank[5][:, 0:N]).then_inc(S["ct_read"], 1)
            dve.wait_ge(S["ct_read"], 1)
            chain(v.tensor_scalar(mask[:, :], CTs[:, :], 1.0, None, ALU.min))
            dve.wait_ge(S["scores_done"], 1)
            for o in range(2):
                v.tensor_tensor(attn[:, o], (bank[1] if o == 0 else bank[7])[:, :].rearrange("p (j n) -> p j n", j=KC),
                                mask[:, :].unsqueeze(1).to_broadcast([P, KC, N]), ALU.mult).then_inc(S["scores_read"], 1)
            dve.wait_ge(S["scores_read"], 2)
            flat = attn.rearrange("p o j n -> p (o j) n")
            by_node = attn.rearrange("p o j n -> p n (o j)")
            top = small_n[:, 0, :]
            chain(v.tensor_reduce(top, by_node, AX.X, ALU.max))
            v.tensor_tensor(flat, flat, top.unsqueeze(1).to_broadcast([P, HEADS, N]), ALU.subtract).then_inc(S["s_centred"], 1)
            dve.wait_ge(S["v_done"], 1)
            dve.wait_ge(row_out, 1)
            v.tensor_tensor(v_sb, bank[4][:, :], r("L0_gnn_bv"), ALU.add).then_inc(S["v_ready"], 1)
            chain(v.tensor_reduce(small[:, 0:1], CTs[:, :], AX.X, ALU.add))
            v.tensor_scalar(small[:, 1:2], small[:, 0:1], 1.0, None, ALU.add).then_inc(S["deg_ready"], 1)
            chain(v.tensor_scalar(small[:, 3:4], small[:, 0:1], 1.0, None, ALU.max))
            chain(v.reciprocal(small[:, 4:5], small[:, 3:4]))
            v.tensor_scalar(Cn[:, :], CTs[:, :], small[:, 4:5], None, ALU.mult).then_inc(S["graphT_ready"], 1)
            chain(v.tensor_tensor(mask[:, :], CTs[:, :], ident[:, :], ALU.add))
            dve.wait_ge(S["exp_done"], 1)
            total = small_n[:, 1, :]
            chain(v.tensor_reduce(total, by_node, AX.X, ALU.add))
            chain(v.reciprocal(total, total))
            v.tensor_tensor(flat, flat, total.unsqueeze(1).to_broadcast([P, HEADS, N]), ALU.mult).then_inc(S["attn_ready"], 1)
            dve.wait_ge(row_out, 8)
            chain(v.tensor_tensor(xw[:, :], xs[:, :], r("L0_gnn_bo"), ALU.add))
            chain(v.tensor_tensor(xb, xs[:, :], r("L0_gnn_be2"), ALU.add))
            dve.wait_ge(S["ao_done"], 1)
            v.tensor_copy(aoT.rearrange("p c n -> p (c n)"), bank[2][:, :]).then_inc(S["ao_ready"], 1)
            dve.wait_ge(S["dinv_ready"], 1)
            v.tensor_scalar(Ahat[:, :], mask[:, :], small[:, 2:3], None, ALU.mult).then_inc(S["graphT_ready"], 1)
            dve.wait_ge(S["wc_in"], 32)
            chain(v.tensor_copy(Chi[:, :], Wc_raw[:, :]))
            v.tensor_tensor(Clo[:, :], Wc_raw[:, :], Chi[:, :].bitcast(F32), ALU.subtract).then_inc(S["c_split"], 1)
            dve.wait_ge(S["bc_ready"], 2)
            node_hot(DT, dst_bc)
            dve.wait_ge(S["c_split"], 1)
            dve.wait_ge(S["wo_done"], 1)
            chain(v.tensor_tensor(y[:, :], bank[3][:, :], xw[:, :], ALU.add))
            norm_gain(y[:, :], y[:, :], r("L0_gnn_g1"), r("L0_gnn_be1")).then_inc(S["nx_ready"], 1)
            dve.wait_ge(S["nT_done"], 1)
            v.tensor_copy(xT[:, :, :].rearrange("p c n -> p (c n)"), bank[1][:, :]).then_inc(S["nT_ready"], 1)
            dve.wait_ge(S["nx_ready"], 1)
            chain(v.tensor_tensor(xw[:, :], y[:, :], r("L0_gnn_b2"), ALU.add))
            dve.wait_ge(S["graphT_done"], 1)
            v.tensor_scalar(Ahat[:, :], bank[7][:, 0:N], small[:, 2:3], None, ALU.mult).then_inc(S["graph_ready"], 1)
            v.tensor_copy(Cn[:, :], bank[7][:, N:2 * N]).then_inc(S["graph_ready"], 1)
            dve.wait_ge(S["f2_done"], 1)
            chain(v.tensor_tensor(y[:, :], bank[3][:, :], xw[:, :], ALU.add))
            chain(norm_gain(y[:, :], y[:, :], r("L0_gnn_g2"), xb))
            norm(y[:, :], xs[:, :]).then_inc(S["nx_ready"], 2)
            dve.wait_ge(S["nT_done"], 2)
            v.tensor_copy(xT[:, :, :].rearrange("p c n -> p (c n)"), bank[1][:, :]).then_inc(S["nT_ready"], 1)
            for i, (hi, lo, b) in enumerate(((Ahi, Alo, bank[2]), (Bhi, Blo, bank[4]))):
                dve.wait_ge(S["ab_done"], i + 1)
                v.tensor_copy(hi[:, :], b[:, :]).then_inc(S["ab_ready"], 1)
                dve.wait_ge(S["ab_ready"], 2 * i + 1)
                v.tensor_tensor(lo[:, :], b[:, :], hi[:, :].bitcast(F32), ALU.subtract).then_inc(S["ab_ready"], 1)

            def z1_out(g, j):
                dve.wait_ge(S["z1_done"], units(g, j) + 1)
                if j == 0 and g >= 2:
                    dve.wait_ge(S["h_lo"], 2 * (g - 1))
                c = col["L1_gnn_b1"] + j
                v.tensor_scalar(z1(g)[:, j, :], ST1[units(g, j) % 3][:, :], cols[:, c:c + 1], None, ALU.add).then_inc(S["z1_read"], 1)

            def z1_out_half(h, j):
                u = KC * h + j
                dve.wait_ge(S["z1_done"], u + 1)
                c = col["L1_gnn_b1"] + j
                v.tensor_scalar(z1(0)[:, j, GE // 2 * h:GE // 2 * (h + 1)], ST1[u % 3][:, 0:GE // 2], cols[:, c:c + 1], None,
                                ALU.add).then_inc(S["z1_read"], 1)

            def z2_out(g, t):
                dve.wait_ge(S["z2_done"], GT * g + t + 1)
                if t == 0 and g >= 2:
                    dve.wait_ge(S["m_lo"], 2 * (g - 1))
                v.tensor_tensor(z2(g)[:, t, :], ST2[t][:, :], r("L1_gnn_b2"), ALU.add).then_inc(S["z2_read"], 1)

            def h_product(g, h):
                e = slice(GE // 2 * h, GE // 2 * (h + 1))
                dve.wait_ge(S["tanh1"], 2 * g + h + 1)
                v.tensor_tensor(z1(g)[:, :, e], z1(g)[:, :, e], T1[:, :, e], ALU.mult).then_inc(S["h_mul"], 1)

            def h_high(g, h):
                e = slice(GE // 2 * h, GE // 2 * (h + 1))
                dve.wait_ge(S["h_mul"], 2 * g + h + 1)
                if g >= 2:
                    dve.wait_ge(S["z2_done"], GT * (g - 1))
                v.tensor_copy(Hhi[:, g % 2, :, e], z1(g)[:, :, e]).then_inc(S["h_hi"], 1)
                if g == 0:
                    dve.wait_ge(S["h_hi"], h + 1)
                    v.tensor_tensor(Hlo[:, 0, :, e], z1(0)[:, :, e], Hhi[:, 0, :, e].bitcast(F32), ALU.subtract).then_inc(S["h_lo"], 1)

            def m_product(g, h):
                t = slice(2 * h, 2 * (h + 1))
                dve.wait_ge(S["tanh2"], 2 * g + h + 1)
                v.tensor_tensor(z2(g)[:, t, :], z2(g)[:, t, :], (T1 if g == G - 1 else T2)[:, t, :], ALU.mult).then_inc(S["m_mul"], 1)

            def one_hot(g):
                if g >= 1:
                    dve.wait_ge(S["agg_done"], g)
                v.tensor_tensor(Dg[:, :, :], dcol[:, GT * g:GT * (g + 1)].unsqueeze(2).to_broadcast([P, GT, N]),
                                iota_row[:, :].unsqueeze(1).to_broadcast([P, GT, N]), ALU.is_equal).then_inc(S["m_oh"], 1)

            def m_high(g, h):
                t = slice(2 * h, 2 * (h + 1))
                dve.wait_ge(S["m_mul"], 2 * g + h + 1)
                v.tensor_copy(Mhi[:, t, :], z2(g)[:, t, :]).then_inc(S["m_hi"], 1)
                if g == G - 1 and h == 1:
                    dve.wait_ge(S["m_hi"], 2 * g + h + 1)
                    v.tensor_tensor(Mlo[:, t, :], z2(g)[:, t, :], Mhi[:, t, :].bitcast(F32), ALU.subtract).then_inc(S["m_lo_last"], 1)

            for s in range(G + LAG2 + 1):
                gh, g2, gm = s - 1, s - LAG2, s - 1 - LAG2
                if s == 0:
                    for i in range(2 * KC):
                        z1_out_half(i // KC, i % KC)
                elif s < G:
                    for j in range(KC):
                        z1_out(s, j)
                late = s >= G
                if 0 <= gh < G:
                    h_product(gh, 0)
                    h_high(gh, 0)
                if 0 <= g2 < G:
                    z2_out(g2, 0)
                if 0 <= gh < G:
                    h_product(gh, 1)
                    h_high(gh, 1)
                if 0 <= g2 < G:
                    z2_out(g2, 1)
                    if late:
                        z2_out(g2, 2)
                        z2_out(g2, 3)
                if gm >= 0:
                    if gm == G - 1:
                        for q in range(2 * KC):
                            dve.wait_ge(S["wt_done"], q + 1)
                            if q == 0:
                                dve.wait_ge(S["z2_done"], GT * G)
                            v.tensor_copy((WsT if q < KC else WnT)[:, q % KC, :], bank[3 + q % 2][:, :]).then_inc(S["wt_ready"], 1)
                        one_hot(gm)
                    m_product(gm, 0)
                if 0 <= g2 < G and not late:
                    z2_out(g2, 2)
                if gm == G - 1:
                    m_high(gm, 0)
                if gm >= 0:
                    m_product(gm, 1)
                if 0 <= g2 < G and not late:
                    z2_out(g2, 3)
                if gm >= 0:
                    if gm < G - 1:
                        one_hot(gm)
                        m_high(gm, 0)
                    m_high(gm, 1)
            dve.wait_ge(S["ux_done"], 1)
            c = col["L1_gnn_b3"]
            v.tensor_tensor(chunks(ux, KC), bank[7][:, :].rearrange("p (j n) -> p j n", j=KC),
                            cols[:, c:c + KC].unsqueeze(2).to_broadcast([P, KC, N]), ALU.add).then_inc(S["ux_ready"], 1)
            dve.wait_ge(row_out, 15)
            chain(v.tensor_tensor(xw[:, :], xs[:, :], r("L1_gnn_b4"), ALU.add))
            chain(v.tensor_tensor(xb_late, xs[:, :], r("L1_gnn_beta"), ALU.add))
            dve.wait_ge(S["agg_done"], G)
            v.tensor_copy(agg_sb, AGG[:, :]).then_inc(S["agg_ready"], 1)
            dve.wait_ge(S["aggT_done"], 1)
            v.tensor_copy(aggT.rearrange("p c n -> p (c n)"), bank[1][:, :]).then_inc(S["aggT_ready"], 1)
            dve.wait_ge(S["u_done"], 1)
            dve.wait_ge(S["ux_ready"], 1)
            v.tensor_tensor(zu, bank[2][:, :], ux, ALU.add).then_inc(S["zu_ready"], 1)
            dve.wait_ge(S["u_act"], 1)
            v.tensor_tensor(uT.rearrange("p c n -> p (c n)"), zu, tu, ALU.mult).then_inc(S["u_ready"], 1)
            dve.wait_ge(S["o_done"], 1)
            chain(v.tensor_tensor(y[:, :], bank[5][:, :], xw[:, :], ALU.add))
            chain(norm_gain(y[:, :], y[:, :], r("L1_gnn_gamma"), xb_late))
            norm(y[:, :], xs[:, :]).then_inc(S["nx_ready"], 2)
            dve.wait_ge(S["g0_done"], 1)
            v.tensor_copy(xT[:, :, :].rearrange("p c n -> p (c n)"), bank[1][:, :]).then_inc(S["g0_ready"], 1)
            dve.wait_ge(S["nx_ready"], 5)
            chain(v.tensor_tensor(xw[:, :], xs[:, :], r("L2_gnn_b2"), ALU.add))
            dve.wait_ge(S["g1_done"], 1)
            dve.wait_ge(S["b1g_in"], 16)
            chain(v.tensor_tensor(r1g, bank[3][:, 0:HID2], b1g[:, :], ALU.add))
            v.tensor_scalar(r1g, r1g, 0.0, None, ALU.max).then_inc(S["g1_ready"], 1)
            dve.wait_ge(S["g2_done"], 1)
            v.tensor_copy(p1g, bank[4][:, 0:N]).then_inc(S["g2_ready"], 1)
            dve.wait_ge(S["g3_done"], 1)
            chain(v.tensor_tensor(y[:, :], bank[5][:, :], xw[:, :], ALU.add))
            norm(y[:, :], xs[:, :]).then_inc(S["nx_ready"], 1)
            dve.wait_ge(S["nT_done"], 3)
            v.tensor_copy(xT[:, :, :].rearrange("p c n -> p (c n)"), bank[1][:, :]).then_inc(S["nT_ready"], 1)
            dve.wait_ge(S["nm_done"], 1)
            v.tensor_copy(nmT.rearrange("p c n -> p (c n)"), bank[2][:, :]).then_inc(S["nm_ready"], 1)
            dve.wait_ge(S["nx_ready"], 6)
            chain(v.tensor_tensor(xs[:, :], xs[:, :], r("L3_gnn_beta"), ALU.add))
            dve.wait_ge(S["l3_done"], 1)
            chain(v.tensor_tensor(y[:, :], bank[6][:, :], r("L3_gnn_bias"), ALU.add))
            chain(norm_gain(y[:, :], y[:, :], r("L3_gnn_gamma"), xs[:, :]))
            norm(y[:, :], y[:, :]).then_inc(S["y_final"], 1)


def kernel(**inputs):
    import numpy as np
    import concourse.bacc as bacc
    from concourse import mybir as mb
    from concourse.bass_utils import run_bass_kernel_spmd as run

    nc = bacc.Bacc("TRN2", target_bir_lowering=False, num_devices=1)
    arrays, args = {}, {}
    for name, value in inputs.items():
        v = np.ascontiguousarray(value)
        arrays[f"in_{name}"] = v
        args[name] = nc.dram_tensor(f"in_{name}", v.shape, mb.dt.from_np(v.dtype), kind="ExternalInput").ap()
    out = nc.dram_tensor("out_0", (N, D), F32, kind="ExternalOutput").ap()
    gnn_kernel(nc, args, out)
    r = run(nc, [arrays], core_ids=[0])
    return r.results[0]["out_0"]
```

```python
import concourse.bass as bass
from concourse import mybir
from contextlib import ExitStack

F32 = mybir.dt.float32
F32R = mybir.dt.float32r
BF16 = mybir.dt.bfloat16
I32 = mybir.dt.int32
ALU = mybir.AluOpType
ACT = mybir.ActivationFunctionType
AX = mybir.AxisListType

P = 128
N = 128
D = 512
KC = D // P
E = 4096
ET = E // P
EDIM = 64
HEADS = 8
HEAD = D // HEADS
FF = 2 * D
FC = FF // P
HID2 = 128
EPS = 1e-5
GT = 4
GE = GT * P
G = E // GE
LAG2 = 2
LAG3 = 4
HALF = KC * GE
TINY = 2.0 ** -63
TOP = 16.0

ROWS = ["L0_gnn_bv", "L0_gnn_bo", "L0_gnn_g1", "L0_gnn_be1", "L0_gnn_b2", "L0_gnn_g2", "L0_gnn_be2",
        "L1_gnn_b2", "L1_gnn_b4", "L1_gnn_gamma", "L1_gnn_beta", "L2_gnn_b2",
        "L3_gnn_bias", "L3_gnn_gamma", "L3_gnn_beta"]
COLS = [("L0_gnn_bq", KC), ("L0_gnn_bk", KC), ("L0_gnn_b1", FC), ("L1_gnn_b1", KC), ("L1_gnn_b3", KC)]


def gnn_kernel(nc, a, out):
    ctx = ExitStack()
    with ctx:
        def sb(name, shape, dt=F32):
            return ctx.enter_context(nc.sbuf_tensor(name, shape, dt))

        def sem(name):
            return ctx.enter_context(nc.semaphore(name))

        Z = sb("Z", [P, 2, 2 * HALF])
        T = sb("T", [P, 2 * HALF])
        Dg = sb("Dg", [P, GT, N], F32R)
        Chi = sb("Chi", [P, D], F32R)
        Clo = sb("Clo", [P, D], F32R)
        rows = sb("rows", [P, 8, D])
        vecs = sb("vecs", [24, P])
        cols = sb("cols", [P, 24])
        b1g = sb("b1g", [P, HID2])
        xs = sb("xs", [P, D])
        xT = sb("xT", [P, KC, N])
        xw = sb("xw", [P, D])
        y = sb("y", [P, D])
        iota_row = sb("iota_row", [P, P])
        iota_col = sb("iota_col", [P, 1])
        ident = sb("ident", [P, P])
        dcol = sb("dcol", [P, ET], I32)
        scol = sb("scol", [P, ET], I32)
        Ahat = sb("Ahat", [P, N])
        Cn = sb("Cn", [P, N])
        CTs = sb("CTs", [P, N])
        mask = sb("mask", [P, N])
        small = sb("small", [P, 16])
        stats = sb("stats", [P, 2, 6])
        mv = sb("mv", [P, 2])
        rstd = sb("rstd", [P, 1])
        mhalf = sb("mhalf", [P, 1])
        tiny = sb("tiny", [P, 1])
        ones = sb("ones", [P, 1])
        small_n = sb("small_n", [P, 2, N])

        Z0, Z1 = Z[:, 0, :], Z[:, 1, :]

        def chunks(v, k):
            return v.rearrange("p (c n) -> p c n", c=k)

        def stage(*tensors):
            with ExitStack() as st:
                made = []
                for name, words, dt in tensors:
                    t = st.enter_context(nc.sbuf_tensor(name, [P, words], dt))
                    made.append(t[:, :])
            return [t for t, (name, _, _) in zip(made, tensors) if not name.startswith("pad")]

        W = KC * D
        Wq, Wk, Wv, Wo, MA, MB, Dbf, Sbf, ea_raw, rowvec8, idrow0 = stage(
            ("Wq", W, F32), ("Wk", W, F32), ("Wv", W, F32), ("Wo", W, F32), ("MA", W, F32), ("MB", W, F32),
            ("Dbf", 2 * W, BF16), ("Sbf", 2 * W, BF16), ("ea_raw", W, F32), ("pad0", E, F32), ("rowvec8", E, F32), ("idrow", E, I32))
        Hhi, Hlo, Mhi, Mlo, W2hi, W2lo, Ahi, Alo, Bhi, Blo, ST, DT, EAT = stage(
            ("Hhi", 2 * W, F32R),
            ("Hlo", 2 * W, F32R),
            ("Mhi", W, F32R), ("Mlo", W, F32R),
            ("W2hi", W, F32R), ("W2lo", W, F32R),
            ("Ahi", D, F32R), ("Alo", D, F32R), ("Bhi", D, F32R), ("Blo", D, F32R),
            ("ST", E, F32R), ("DT", E, F32R),
            ("EAT", E, F32R))
        WsT, WnT, tail, WsR, WnR, W4, G1, G2, W3 = stage(
            ("WsT", W, F32), ("WnT", W, F32), ("tail", 2 * W, F32), ("pad1", 5 * W, F32),
            ("WsR", W, F32), ("WnR", W, F32), ("W4", W, F32), ("G1", D, F32), ("G2", D, F32),
            ("pad2", 2 * D, F32), ("W3", 2 * W, F32))
        stage_bytes = ctx.enter_context(nc.sbuf_tensor("stages", [P, 15 * W], F32))

        Wq, Wk, Wv, Wo, W4, WsR, WnR, WsT, WnT, G1 = (chunks(w, KC) for w in (Wq, Wk, Wv, Wo, W4, WsR, WnR, WsT, WnT, G1))
        W2hi, W2lo = chunks(W2hi, KC), chunks(W2lo, KC)
        W1hi, W1lo = chunks(Hhi, 2 * KC), chunks(Hlo, 2 * KC)
        xhi, xlo = chunks(Mhi[:, 0:D], KC), chunks(Mlo[:, 0:D], KC)
        W3 = chunks(W3, 2 * KC)
        Hhi, Hlo = (h.rearrange("p (a k n) -> p a k n", a=2, k=KC) for h in (Hhi, Hlo))
        Mhi, Mlo = chunks(Mhi, GT), chunks(Mlo, GT)
        Dbf, Sbf = chunks(Dbf, ET), chunks(Sbf, ET)
        W2raw = chunks(ea_raw, KC)
        ea_raw = chunks(ea_raw, ET)
        F1 = chunks(T[:, :], KC)
        F2 = chunks(Z0, FC)
        src_bc, dst_bc = Z0.bitcast(I32), Z1.bitcast(I32)
        EAs = chunks(Z0, ET)
        W1ab = chunks(Z1, 2 * KC)
        qT = chunks(MA[:, 0:D], KC)
        kT = chunks(MA[:, D:2 * D], KC)
        v_sb = MA[:, 2 * D:3 * D]
        aoT = chunks(MA[:, 3 * D:4 * D], KC)
        attn = MB[:, 0:2 * D].rearrange("p (o j n) -> p o j n", o=2, j=KC)
        ffT = chunks(MB[:, 2 * D:4 * D], FC)
        xb = MA[:, D:2 * D]
        xb_late = tail[:, 7 * D:8 * D]
        Dg6, Dg7 = chunks(y[:, :], GT), chunks(xw[:, :], GT)
        Wc_raw = MB[:, 2 * D:3 * D]
        idrow = [idrow0[0:1, :], T[0:1, :].bitcast(I32)]
        rowvec8 = chunks(rowvec8[0:1, :], 8)
        rowvec = sb("rowvec", [1, 2, D])
        ux = tail[:, 0:D]
        zu = tail[:, D:2 * D]
        tu = tail[:, 2 * D:3 * D]
        uT = chunks(tail[:, 3 * D:4 * D], KC)
        aggT = chunks(tail[:, 4 * D:5 * D], KC)
        agg_sb = tail[:, 5 * D:6 * D]
        r1g = tail[:, 6 * D + HID2:6 * D + 2 * HID2]
        p1g = tail[:, 6 * D + 2 * HID2:6 * D + 3 * HID2]
        nmT = chunks(tail[:, 7 * D:8 * D], KC)

        bank = [ctx.enter_context(nc.psum_tensor(f"bank{i}", [P, D], F32)) for i in range(8)]
        AGG, ST1, ST2 = bank[0], [bank[1], bank[2], bank[7]], bank[3:7]

        TURN = (bank[3], bank[4], bank[6], bank[0])

        def half(v, h):
            return v[:, D // 2 * h:D // 2 * (h + 1)]

        def quarter(b, j):
            return b[:, P * j:P * (j + 1)]

        col = {}
        at = 0
        for name, k in COLS:
            col[name] = at
            at += k
        slot = {name: i % 8 for i, name in enumerate(ROWS)}

        S = {}
        for name in ("x_in ids_in vecs_in ea_in wq_in wk_in wv_in wo_in f1_in f2_in w1ab_in wc_in w2_in w3_in w4_in g_in ws_in wn_in b1g_in "
                     "out_stored consts ident_ready x_transposed xT_ready cols_done cols_ready q_done k_done v_done "
                     "qk_ready v_ready onehot_bf ct_done ct_read scores_done scores_read s_centred exp_done attn_ready ao_done ao_ready wo_done "
                     "stat_ready rstd_ready nx_ready nT_done nT_ready f1_done ff_ready f2_done "
                     "src_row dst_row bc_ready st_ready xw_ready ea_hi ea_split ea_T ea_Tready w2_hi w2_split w1_hi w1_lo xs_hi xs_lo c_split ab_done ab_ready "
                     "graphT_ready graphT_done graph_ready deg_ready dinv_ready "
                     "z1_done z1_read z2_done z2_read sig1 sig2 log1 log2 tanh1 tanh2 h_mul h_hi h_lo m_mul m_hi m_lo m_oh oh_late late_top late_exp late_log late_tanh late_mul agg_done "
                     "ux_done ux_ready agg_ready aggT_done aggT_ready u_done zu_ready u_act u_ready o_done "
                     "g0_done g0_ready g1_done g1_ready g2_done g2_ready g3_done nm_done nm_ready l3_done wt_done wt_ready y_final "
                     "dve_chain act_chain").split():
            S[name] = sem(name)
        row_in = [sem(f"row_in{i}") for i in range(10)]
        row_out = sem("row_out")

        block = ctx.enter_context(nc.Block())

        def w_view(w):
            return w.rearrange("(c p) n -> p c n", p=P)

        def hop(eng, name):
            n = [0]

            def link(ins):
                n[0] += 1
                ins.then_inc(S[name], 1)
                eng.wait_ge(S[name], n[0])
            return link

        def z1(g):
            return chunks(Z[:, g % 2, 0:HALF], KC)

        def z2(g):
            return chunks(Z[:, g % 2, 0:HALF] if g == G - 1 else Z[:, g % 2, HALF:], GT)

        def units(g, j=0):
            return KC * g + j + (KC if g else 0)

        T1, T2 = chunks(T[:, 0:HALF], KC), chunks(T[:, HALF:], GT)

        @block.sync
        def _(sp):
            sp.dma_start(xs[:, :], a["x"]).then_inc(S["x_in"], 16)
            sp.dma_start(dcol[:, :], a["dst"].rearrange("(p t) -> p t", p=P)).then_inc(S["ids_in"], 16)
            sp.dma_start(Wq, w_view(a["L0_gnn_Wq"])).then_inc(S["wq_in"], 16)
            sp.dma_start(Wk, w_view(a["L0_gnn_Wk"])).then_inc(S["wk_in"], 16)
            sp.wait_ge(S["vecs_in"], 16 * len(COLS))
            sp.dma_start(ea_raw, a["edge_attr_64"].rearrange("(p t) n -> p t n", p=P)).then_inc(S["ea_in"], 16)
            sp.dma_start(Wv, w_view(a["L0_gnn_Wv"])).then_inc(S["wv_in"], 16)
            sp.dma_start(Wo, w_view(a["L0_gnn_Wo"])).then_inc(S["wo_in"], 16)
            sp.wait_ge(S["bc_ready"], 2)
            sp.dma_start(F1, w_view(a["L0_gnn_W1"])).then_inc(S["f1_in"], 16)
            sp.wait_ge(S["ea_split"], 1)
            sp.dma_start(W2raw, w_view(a["L1_gnn_W2"])).then_inc(S["w2_in"], 16)
            sp.wait_ge(S["ea_T"], 8)
            sp.dma_start(F2, w_view(a["L0_gnn_W2"])).then_inc(S["f2_in"], 16)
            sp.wait_ge(S["st_ready"], 2)
            sp.dma_start(W1ab, w_view(a["L1_gnn_W1"][0:2 * D, :])).then_inc(S["w1ab_in"], 16)
            for i in range(8, 15):
                if i >= 10:
                    sp.wait_ge(row_out, i - 1)
                sp.dma_start(rowvec[0:1, i % 2, :], a[ROWS[i]].rearrange("(o n) -> o n", o=1)).then_inc(row_in[8 + i % 2], 16)
            sp.wait_ge(S["z1_done"], units(G))
            sp.dma_start(W3, w_view(a["L1_gnn_W3"])).then_inc(S["w3_in"], 16)
            sp.dma_start(W4, w_view(a["L1_gnn_W4"])).then_inc(S["w4_in"], 16)
            sp.dma_start(G1, w_view(a["L2_gnn_W1"])).then_inc(S["g_in"], 16)
            sp.dma_start(G2, a["L2_gnn_W2"]).then_inc(S["g_in"], 16)
            sp.dma_start(WsR, w_view(a["L3_gnn_W_self"])).then_inc(S["ws_in"], 16)
            sp.dma_start(WnR, w_view(a["L3_gnn_W_neigh"])).then_inc(S["wn_in"], 16)
            for h in range(2):
                sp.wait_ge(S["y_final"], h + 1)
                sp.dma_start(half(out, h), half(y, h)).then_inc(S["out_stored"], 16)
            sp.wait_ge(S["out_stored"], 32)

        @block.gpsimd
        def _(pool):
            pool.iota(iota_row[:, :], pattern=[[1, P]], base=0, channel_multiplier=0,
                      allow_small_or_imprecise_dtypes=True).then_inc(S["consts"], 1)
            pool.iota(iota_col[:, :], pattern=[[0, 1]], base=0, channel_multiplier=1,
                      allow_small_or_imprecise_dtypes=True).then_inc(S["consts"], 1)
            pool.memset(mhalf[:, :], -0.5).then_inc(S["consts"], 1)
            pool.wait_ge(S["consts"], 3)

            def row(i):
                if i < 8:
                    pool.wait_ge(row_in[i], 16)
                    src = rowvec8[:, i, :]
                else:
                    pool.wait_ge(row_in[8 + i % 2], 16 * (i // 2 - 3))
                    src = rowvec[0:1, i % 2, :]
                pool.partition_broadcast(rows[:, slot[ROWS[i]], :], src).then_inc(row_out, 1)

            def inverse_root(k, src, dst, ready, signal):
                pool.wait_ge(ready, k)
                pool.tensor_tensor(dst, src, mhalf[:, :], ALU.pow).then_inc(signal, 1)

            norms = [0]

            def norm():
                norms[0] += 1
                inverse_root(norms[0], mv[:, 1:2], rstd[:, :], S["stat_ready"], S["rstd_ready"])

            pool.wait_ge(S["src_row"], 16)
            pool.partition_broadcast(src_bc, idrow[0]).then_inc(S["bc_ready"], 1)
            pool.wait_ge(S["dst_row"], 16)
            pool.partition_broadcast(dst_bc, idrow[1]).then_inc(S["bc_ready"], 1)
            row(0)
            pool.wait_ge(S["ea_hi"], 1)
            pool.tensor_tensor(EAs[:, :, EDIM:], ea_raw, EAs[:, :, 0:EDIM], ALU.subtract).then_inc(S["ea_split"], 1)
            for i in range(1, 8):
                row(i)
            norm()
            inverse_root(1, small[:, 1:2], small[:, 2:3], S["deg_ready"], S["dinv_ready"])
            pool.wait_ge(S["w2_hi"], 1)
            pool.tensor_tensor(W2lo[:, :, :], W2raw, W2hi.bitcast(F32), ALU.subtract).then_inc(S["w2_split"], 1)
            norm()
            norm()
            pool.wait_ge(S["nx_ready"], 4)
            for i in range(8, 15):
                row(i)

            def low(dst, z, high, signal):
                pool.tensor_tensor(dst, z, high.bitcast(F32), ALU.subtract).then_inc(signal, 1)

            for s in range(G + LAG2):
                if 1 <= s < G:
                    for h in range(2):
                        pool.wait_ge(S["h_hi"], 2 * s + h + 1)
                        e = slice(GE // 2 * h, GE // 2 * (h + 1))
                        low(Hlo[:, s % 2, :, e], z1(s)[:, :, e], Hhi[:, s % 2, :, e], S["h_lo"])
                if s >= LAG2:
                    g = s - LAG2
                    if g >= G - 2:
                        continue
                    for h in range(2):
                        pool.wait_ge(S["m_hi"], 2 * g + h + 1)
                        t = slice(GT // 2 * h, GT // 2 * (h + 1))
                        low(Mlo[:, t, :], z2(g)[:, t, :], Mhi[:, t, :], S["m_lo"])
            for _ in range(5):
                norm()

        @block.scalar
        def _(act):
            act.dma_start(scol[:, :], a["src"].rearrange("(p t) -> p t", p=P)).then_inc(S["ids_in"], 16)
            act.dma_start(idrow[0], a["src"].rearrange("(o n) -> o n", o=1)).then_inc(S["src_row"], 16)
            act.dma_start(idrow[1], a["dst"].rearrange("(o n) -> o n", o=1)).then_inc(S["dst_row"], 16)
            for name, k in COLS:
                act.dma_start(vecs[col[name]:col[name] + k, :], a[name].rearrange("(k p) -> k p", p=P)).then_inc(S["vecs_in"], 16)
            for i in range(8):
                act.dma_start(rowvec8[:, i, :], a[ROWS[i]].rearrange("(o n) -> o n", o=1)).then_inc(row_in[i], 16)
            for h in range(2):
                act.dma_start(Wc_raw[EDIM * h:EDIM * (h + 1), :], a["L1_gnn_W1"][2 * D:, :]).then_inc(S["wc_in"], 16)
            act.dma_start(b1g[:, :], a["L2_gnn_b1"].rearrange("(o n) -> o n", o=1).to_broadcast([P, HID2])).then_inc(S["b1g_in"], 16)

            def bias_out(dst, src, name, j, func=ACT.Identity):
                return act.activation(dst, src, func, bias=cols[:, col[name] + j:col[name] + j + 1])

            act.wait_ge(S["cols_done"], 1)
            act.activation(cols[:, :], bank[7][:, 0:24], ACT.Copy).then_inc(S["cols_ready"], 1)
            act.wait_ge(S["cols_ready"], 1)
            act.wait_ge(S["q_done"], 1)
            for j in range(KC):
                bias_out(qT[:, j, :], quarter(bank[2], j), "L0_gnn_bq", j).then_inc(S["qk_ready"], 1)
            act.wait_ge(S["k_done"], 1)
            for j in range(KC):
                bias_out(kT[:, j, :], quarter(bank[3], j), "L0_gnn_bk", j).then_inc(S["qk_ready"], 1)
            act.wait_ge(S["ea_in"], 16)
            act.wait_ge(S["st_ready"], 1)
            act.activation(EAs[:, :, 0:EDIM].bitcast(F32R), ea_raw, ACT.Copy).then_inc(S["ea_hi"], 1)
            for o in range(2):
                act.wait_ge(S["s_centred"], o + 1)
                act.activation(attn[:, o].rearrange("p j n -> p (j n)"), attn[:, o].rearrange("p j n -> p (j n)"), ACT.Exp,
                               scale=float(HEAD) ** -0.5).then_inc(S["exp_done"], 1)
            for q in range(ET // 4):
                act.wait_ge(S["ea_T"], q + 1)
                act.activation(EAT[:, 4 * P * q:4 * P * (q + 1)], bank[5 + q % 2][:, :], ACT.Copy).then_inc(S["ea_Tready"], 1)
            act.wait_ge(S["w2_in"], 16)
            act.activation(W2hi[:, :, :], W2raw, ACT.Copy).then_inc(S["w2_hi"], 1)
            act.wait_ge(S["c_split"], 1)

            def w1_high(i):
                act.wait_ge(S["w1ab_in"], 16)
                act.wait_ge(S["wo_done"], 2)
                act.activation(W1hi[:, 2 * i:2 * i + 2, :], W1ab[:, 2 * i:2 * i + 2, :], ACT.Copy).then_inc(S["w1_hi"], 1)

            for i in range(4):
                act.wait_ge(S["f1_done"], i + 1)
                for j in (2 * i, 2 * i + 1):
                    bias_out(ffT[:, j, :], quarter((bank[2], bank[4], bank[5], bank[6])[i], j % 2), "L0_gnn_b1", j,
                             ACT.Relu).then_inc(S["ff_ready"], 1)
                if i >= 1:
                    w1_high(i - 1)
            w1_high(3)
            def mish(g1, g2):
                if g1 is not None:
                    act.wait_ge(S["z1_read"], units(g1 + 1))
                    if g1 >= 1:
                        act.wait_ge(S["h_mul"], 2 * g1)
                    act.activation(T1, z1(g1), ACT.Sigmoid, scale=-1.0).then_inc(S["sig1"], 1)
                if g2 is not None:
                    for h in range(2):
                        act.wait_ge(S["z2_read"], GT * g2 + 2 * (h + 1))
                        if g2 >= 1:
                            act.wait_ge(S["m_mul"], 2 * g2 - 1 + h)
                        t = slice(2 * h, 2 * (h + 1))
                        act.activation(T2[:, t, :], z2(g2)[:, t, :], ACT.Sigmoid, scale=-1.0).then_inc(S["sig2"], 1)
                if g1 is not None:
                    act.wait_ge(S["sig1"], g1 + 2)
                    act.activation(T1, T1, ACT.Ln, bias=tiny[:, 0:1]).then_inc(S["log1"], 1)
                if g2 is not None:
                    act.wait_ge(S["sig2"], 2 * (g2 + 1))
                    act.activation(T2, T2, ACT.Ln, bias=tiny[:, 0:1]).then_inc(S["log2"], 1)
                act.preload_act_table_set("sigmoid_and_others")
                if g1 is not None:
                    act.wait_ge(S["log1"], g1 + 2)
                    for h in range(2):
                        e = slice(GE // 2 * h, GE // 2 * (h + 1))
                        act.activation(T1[:, :, e], T1[:, :, e], ACT.Tanh, scale=-1.0).then_inc(S["tanh1"], 1)
                if g2 is not None:
                    act.wait_ge(S["log2"], g2 + 1)
                    for h in range(2):
                        t = slice(2 * h, 2 * (h + 1))
                        act.activation(T2[:, t, :], T2[:, t, :], ACT.Tanh, scale=-1.0).then_inc(S["tanh2"], 1)

            for h in range(2):
                e = slice(GE // 2 * h, GE // 2 * (h + 1))
                act.wait_ge(S["z1_read"], KC * (h + 1))
                act.activation(T1[:, :, e], z1(0)[:, :, e], ACT.Sigmoid, scale=-1.0).then_inc(S["sig1"], 1)
                act.wait_ge(S["sig1"], h + 1)
                act.activation(T1[:, :, e], T1[:, :, e], ACT.Ln, bias=tiny[:, 0:1]).then_inc(S["log1"], 1)
                act.preload_act_table_set("sigmoid_and_others")
                act.wait_ge(S["log1"], h + 1)
                act.activation(T1[:, :, e], T1[:, :, e], ACT.Tanh, scale=-1.0).then_inc(S["tanh1"], 1)
            for g in range(1, G - 1):
                mish(g, g - LAG2 if g >= LAG2 else None)
            mish(G - 1, None)
            mish(None, G - 3)
            def late(t, tiles, func, before, signal, **bias):
                T = T1 if t < GT else T2
                part = slice(t % GT, t % GT + tiles)
                act.wait_ge(before, t + tiles)
                act.activation(T[:, part, :], T[:, part, :], func, **bias).then_inc(signal, tiles)

            def late_exp(t, tiles):
                late(t, tiles, ACT.Exp, S["late_top"], S["late_exp"])

            def late_log(t, tiles):
                late(t, tiles, ACT.Ln, S["late_exp"], S["late_log"], bias=ones[:, 0:1])

            def late_tanh(t, tiles):
                late(t, tiles, ACT.Tanh, S["late_log"], S["late_tanh"])

            act.preload_act_table_set("natural_log_exp_and_others")
            late_exp(0, 2)
            late_exp(2, 1)
            late_log(0, 2)
            late_exp(3, 1)
            late_log(2, 2)
            late_exp(GT, 1)
            late_log(GT, 1)
            act.preload_act_table_set("exp_and_others")
            late_tanh(0, 2)
            late_tanh(2, 2)
            late_tanh(GT, 1)
            act.preload_act_table_set("natural_log_exp_and_others")
            late_exp(GT + 1, 2)
            late_exp(GT + 3, 1)
            late_log(GT + 1, 2)
            late_log(GT + 3, 1)
            act.preload_act_table_set("exp_and_others")
            for t in range(GT + 1, 2 * GT):
                late_tanh(t, 1)
            act.preload_act_table_set("natural_log_exp_and_others")
            for h in range(2):
                act.wait_ge(S["zu_ready"], h + 1)
                act.activation(half(tu, h), half(tu, h), ACT.Exp).then_inc(S["act_chain"], 1)
                act.wait_ge(S["act_chain"], 2 * h + 1)
                act.activation(half(tu, h), half(tu, h), ACT.Ln, bias=ones[:, 0:1]).then_inc(S["act_chain"], 1)
            act.preload_act_table_set("exp_and_others")
            act.wait_ge(S["act_chain"], 4)
            for h in range(2):
                act.activation(half(tu, h), half(tu, h), ACT.Tanh).then_inc(S["u_act"], 1)
            for q in range(2 * KC):
                if q == 0:
                    act.wait_ge(S["z2_done"], GT * G)
                act.wait_ge(S["wt_done"], q + 1)
                act.activation((WsT if q < KC else WnT)[:, q % KC, :], TURN[q % 4][:, :], ACT.Copy).then_inc(S["wt_ready"], 1)

        @block.tensor
        def _(pe):
            mm = nc.tensor.matmul

            def transpose4(dst, src, signal):
                for c in range(KC):
                    last = nc.tensor.transpose(quarter(dst, c), src[:, P * c:P * (c + 1)], ident[:, :])
                last.then_inc(signal, 1)

            def transpose_halves(banks, src, ready, before, signal):
                for h in range(2):
                    pe.wait_ge(ready, before + h + 1)
                    for c in range(2):
                        last = nc.tensor.transpose(quarter(banks[h], c), src[:, P * (2 * h + c):P * (2 * h + c + 1)], ident[:, :])
                    last.then_inc(signal, 1)

            def nodes_by(dst, lhs, rhs, signal, parts=KC):
                for c in range(parts):
                    last = mm(dst[:, :], lhs[:, c, :], rhs[:, c, :], start=c == 0, stop=c == parts - 1)
                last.then_inc(signal, 1)

            def start_with(banks, x):
                for h in range(2):
                    mm(banks[h][:, 0:D // 2], ident[:, :], half(x, h), start=True, stop=False)

            def columns_by(banks, lhs, rhs, h, cs, first, last):
                for c in cs:
                    done = mm(banks[h][:, 0:D // 2], lhs[:, c, :], rhs[:, c, D // 2 * h:D // 2 * (h + 1)],
                              start=c == first, stop=c == last)
                return done

            def columns_halves(banks, lhs, rhs, ready, before, signal, first=0, last=KC - 1):
                pe.wait_ge(ready, before + 1)
                for h in range(2):
                    columns_by(banks, lhs, rhs, h, (0, 1), first, last)
                pe.wait_ge(ready, before + 2)
                for h in range(2):
                    done = columns_by(banks, lhs, rhs, h, (2, 3), first, last)
                    if signal is not None:
                        done.then_inc(signal, 1)

            def features_by(dst, j0, js, w, rhs, parts, signal, c0=0):
                for j in js:
                    for c in range(parts):
                        last = mm(quarter(dst, j - j0), w[:, c0 + c, P * j:P * (j + 1)], rhs[:, c, :], start=c == 0, stop=c == parts - 1)
                last.then_inc(signal, 1)

            def keep_warm(n, b):
                idle = ident[:, :].bitcast(BF16)
                for _ in range(n):
                    mm(b[:, :], idle[:, 0:P], idle.unsqueeze(1).to_broadcast([P, 2, 2 * P]), start=True, stop=True)

            pe.wait_ge(S["ident_ready"], 1)
            keep_warm(5, bank[2])
            pe.wait_ge(S["x_in"], 16)
            transpose4(bank[1], xs, S["x_transposed"])
            keep_warm(8, bank[2])
            pe.wait_ge(S["xT_ready"], 1)
            pe.wait_ge(S["wq_in"], 16)
            features_by(bank[2], 0, range(KC), Wq, xT, KC, S["q_done"])
            pe.wait_ge(S["vecs_in"], 16 * len(COLS))
            nc.tensor.transpose(bank[7][:, 0:24], vecs[:, :], ident[0:24, 0:24]).then_inc(S["cols_done"], 1)
            pe.wait_ge(S["wk_in"], 16)
            features_by(bank[3], 0, range(KC), Wk, xT, KC, S["k_done"])
            pe.wait_ge(S["onehot_bf"], 2)
            for t in range(ET):
                last = mm(bank[5][:, 0:N], Dbf[:, t, :], Sbf[:, t, :], start=t == 0, stop=t == ET - 1)
            last.then_inc(S["ct_done"], 1)
            pe.wait_ge(S["qk_ready"], 2 * KC)
            for h in range(HEADS):
                o, j = h % 2, h // 2
                part = slice(HEAD * o, HEAD * (o + 1))
                last = mm(quarter(bank[1] if o == 0 else bank[7], j), kT[part, j, :], qT[part, j, :], start=True, stop=True)
            last.then_inc(S["scores_done"], 1)
            pe.wait_ge(S["wv_in"], 16)
            nodes_by(bank[4], xT, Wv, S["v_done"])
            pe.wait_ge(S["ct_read"], 1)
            pe.wait_ge(S["ea_split"], 1)
            for q in range(ET // 4):
                if q >= 2:
                    pe.wait_ge(S["ea_Tready"], q - 1)
                for k in range(4):
                    last = nc.tensor.transpose(quarter(bank[5 + q % 2], k), EAs[:, 4 * q + k, :], ident[:, :])
                last.then_inc(S["ea_T"], 1)
            pe.wait_ge(S["v_ready"], 1)
            for o, j in ((o, j) for o in range(2) for j in range(KC)):
                h = 2 * j + o
                pe.wait_ge(S["attn_ready"], o + 1)
                last = mm(bank[2][HEAD * o:HEAD * (o + 1), P * j:P * (j + 1)], v_sb[:, HEAD * h:HEAD * (h + 1)], attn[:, o, j, :], start=True, stop=True)
            last.then_inc(S["ao_done"], 1)
            pe.wait_ge(S["wo_in"], 16)
            pe.wait_ge(S["xw_ready"], 1)
            pe.wait_ge(S["v_ready"], 1)
            start_with((bank[3], bank[4]), xw)
            columns_halves((bank[3], bank[4]), aoT, Wo, S["ao_ready"], 0, S["wo_done"], None)
            keep_warm(10, bank[1])
            transpose_halves((bank[1], bank[2]), y, S["nx_ready"], 0, S["nT_done"])
            keep_warm(3, bank[4])
            pe.wait_ge(S["nT_ready"], 2)
            pe.wait_ge(S["f1_in"], 16)
            pe.wait_ge(S["ea_Tready"], ET // 4)
            for i, b in enumerate((bank[2], bank[4], bank[5], bank[6])):
                features_by(b, 2 * i, (2 * i, 2 * i + 1), F1, xT, KC, S["f1_done"])
            pe.wait_ge(S["graphT_ready"], 2)
            nc.tensor.transpose(bank[7][:, 0:N], Ahat[:, :], ident[:, :])
            nc.tensor.transpose(bank[7][:, N:2 * N], Cn[:, :], ident[:, :]).then_inc(S["graphT_done"], 1)
            pe.wait_ge(S["f2_in"], 16)
            pe.wait_ge(S["ff_ready"], FC - 2)
            for h in range(2):
                columns_by((bank[3], bank[1]), ffT, F2, h, range(FC - 2), 0, FC - 1)
            pe.wait_ge(S["ff_ready"], FC)
            for h in range(2):
                columns_by((bank[3], bank[1]), ffT, F2, h, range(FC - 2, FC), 0, FC - 1).then_inc(S["f2_done"], 1)
            keep_warm(22, bank[2])
            transpose_halves((bank[1], bank[7]), xs, S["nx_ready"], 2, S["nT_done"])
            keep_warm(3, bank[2])
            pe.wait_ge(S["w1_hi"], 4)
            pe.wait_ge(S["w1_lo"], 4)
            for b, c0 in ((bank[2], 0), (bank[4], KC)):
                for c in range(KC):
                    if c0 == 0 and c % 2 == 0:
                        pe.wait_ge(S["xs_hi"], c // 2 + 1)
                    mm(b[:, :], xhi[:, c, :], W1hi[:, c0 + c, :], start=c == 0, stop=False)
                    mm(b[:, :], xhi[:, c, :], W1lo[:, c0 + c, :], start=False, stop=False)
                for c in range(KC):
                    if c0 == 0 and c % 2 == 0:
                        pe.wait_ge(S["xs_lo"], c // 2 + 1)
                    last = mm(b[:, :], xlo[:, c, :], W1hi[:, c0 + c, :], start=False, stop=c == KC - 1)
                last.then_inc(S["ab_done"], 1)
            pe.wait_ge(S["ab_ready"], 2)
            pe.wait_ge(S["c_split"], 1)
            pe.wait_ge(S["w2_split"], 1)
            terms = [(Chi, EAT), (Clo, EAT), (Ahi, ST), (Alo, ST), (Bhi, DT), (Blo, DT)]

            def first_layer(g, lo=0, hi=KC):
                for j in range(lo, hi):
                    pe.wait_ge(S["z1_read"], units(g, j) - 2)
                    for k, (w, x) in enumerate(terms):
                        last = mm(ST1[units(g, j) % 3][:, :], w[:, P * j:P * (j + 1)], x[:, GE * g:GE * (g + 1)],
                                  start=k == 0, stop=k == len(terms) - 1)
                    last.then_inc(S["z1_done"], 1)

            def first_layer_half(us, ks):
                for u in us:
                    f, edges = slice(P * (u % KC), P * (u % KC + 1)), slice(GE // 2 * (u // KC), GE // 2 * (u // KC + 1))
                    if u >= 3:
                        pe.wait_ge(S["z1_read"], u - 2)
                    for k in ks:
                        w, x = terms[k]
                        last = mm(ST1[u % 3][:, 0:GE // 2], w[:, f], x[:, edges], start=k == 0, stop=k == len(terms) - 1)
                    if k == len(terms) - 1:
                        last.then_inc(S["z1_done"], 1)

            def second_layer(g, h):
                pe.wait_ge(S["h_lo"], 2 * g + h + 1)
                hh, hl = Hhi[:, g % 2], Hlo[:, g % 2]
                for t in (2 * h, 2 * h + 1):
                    if g >= 1:
                        pe.wait_ge(S["z2_read"], GT * (g - 1) + t + 1)
                    e = slice(P * t, P * (t + 1))
                    for c in range(KC):
                        for i, (x, w) in enumerate([(hh, W2hi), (hh, W2lo), (hl, W2hi)]):
                            last = mm(ST2[t][:, :], x[:, c, e], w[:, c, :], start=c == 0 and i == 0, stop=c == KC - 1 and i == 2)
                    last.then_inc(S["z2_done"], 1)

            def sum_messages(g):
                pe.wait_ge(S["m_oh"], g + 1)
                for t in range(GT):
                    pe.wait_ge(S["m_lo"], 2 * g + (1 if t < GT // 2 else 2))
                    mm(AGG[:, :], Dg[:, t, :], Mhi[:, t, :], start=g == 0 and t == 0, stop=False)
                    last = mm(AGG[:, :], Dg[:, t, :], Mlo[:, t, :], start=False, stop=False)
                last.then_inc(S["agg_done"], 1)

            def sum_late(g, t):
                return mm(AGG[:, :], (Dg6 if g == G - 2 else Dg7)[:, t, :], z2(g)[:, t, :], start=False, stop=g == G - 1 and t == GT - 1)

            def turn(q):
                w = WsR if q < KC else WnR
                if q >= 4:
                    pe.wait_ge(S["wt_ready"], q - 3)
                for k in range(KC):
                    last = nc.tensor.transpose(quarter(TURN[q % 4], k), w[:, k, P * (q % KC):P * (q % KC + 1)], ident[:, :])
                last.then_inc(S["wt_done"], 1)

            first_layer_half(range(3), range(4))
            pe.wait_ge(S["ab_ready"], 4)
            first_layer_half(range(2), (4, 5))
            pe.wait_ge(S["ab_ready"], 6)
            first_layer_half((2,), (4, 5))
            first_layer_half(range(3, 2 * KC), range(6))
            first_layer(1)
            first_layer(2, 0, 2)
            second_layer(0, 0)
            first_layer(2, 2, 3)
            second_layer(0, 1)
            first_layer(2, 3, KC)
            for s in range(LAG2 + 1, G + LAG2):
                if s < G:
                    first_layer(s, 0, KC - 1)
                second_layer(s - LAG2, 0)
                if s < G:
                    first_layer(s, KC - 1, KC)
                if LAG3 <= s < G:
                    sum_messages(s - LAG3)
                second_layer(s - LAG2, 1)
                if s == G:
                    sum_messages(s - LAG3)
            sum_messages(G - 3)
            pe.wait_ge(S["w3_in"], 16)
            pe.wait_ge(S["z1_read"], units(G))
            features_by(bank[7], 0, (0, 1), W3, xT, KC, S["ux_done"])
            pe.wait_ge(S["oh_late"], 2)
            for t in range(GT):
                pe.wait_ge(S["late_mul"], t + 1)
                sum_late(G - 2, t)
            for t in range(GT):
                pe.wait_ge(S["late_mul"], GT + t + 1)
                last = sum_late(G - 1, t)
            last.then_inc(S["agg_done"], 1)
            features_by(bank[7], 0, (2,), W3, xT, KC, S["ux_done"])
            transpose_halves((bank[1], bank[3]), agg_sb, S["agg_ready"], 0, S["aggT_done"])
            features_by(bank[7], 0, (3,), W3, xT, KC, S["ux_done"])
            pe.wait_ge(S["aggT_ready"], 2)
            for js in ((0, 1), (2, 3)):
                features_by(bank[5 if js[0] else 2], js[0], js, W3, aggT, KC, S["u_done"], c0=KC)
            pe.wait_ge(S["ws_in"], 16)
            pe.wait_ge(S["z2_read"], GT * G)
            for q in range(KC):
                turn(q)
            pe.wait_ge(S["w4_in"], 16)
            pe.wait_ge(S["xw_ready"], 2)
            pe.wait_ge(S["zu_ready"], 2)
            start_with((bank[1], bank[5]), xw)
            columns_halves((bank[1], bank[5]), uT, W4, S["u_ready"], 0, S["o_done"], None)
            pe.wait_ge(S["wn_in"], 16)
            for q in range(KC, 2 * KC):
                turn(q)
            keep_warm(11, bank[2])
            for j in range(KC):
                pe.wait_ge(S["nx_ready"], 5 + j // 2)
                last = mm(quarter(bank[2], j), xs[:, P * j:P * (j + 1)], Ahat[:, :], start=True, stop=True)
            last.then_inc(S["g0_done"], 1)
            pe.wait_ge(S["wt_ready"], 2 * KC)
            pe.wait_ge(S["b1g_in"], 16)
            mm(bank[3][:, 0:HID2], ident[:, :], b1g[:, :], start=True, stop=False)
            pe.wait_ge(S["g0_ready"], 1)
            pe.wait_ge(S["g_in"], 32)
            for c in range(KC):
                last = mm(bank[3][:, 0:HID2], xT[:, c, :], G1[:, c, :], start=False, stop=c == KC - 1)
            last.then_inc(S["g1_done"], 1)
            pe.wait_ge(S["xw_ready"], 3)
            start_with((bank[5], bank[6]), xw)
            pe.wait_ge(S["g1_ready"], 1)
            mm(bank[4][:, 0:N], r1g, Ahat[:, :], start=True, stop=True).then_inc(S["g2_done"], 1)
            keep_warm(3, bank[1])
            pe.wait_ge(S["g2_ready"], 1)
            for h in range(2):
                mm((bank[5], bank[6])[h][:, 0:D // 2], p1g, half(G2, h), start=False, stop=True).then_inc(S["g3_done"], 1)
            pe.wait_ge(row_out, len(ROWS))
            start_with((bank[4], bank[0]), rows[:, slot["L3_gnn_bias"], :])
            keep_warm(5, bank[1])
            transpose_halves((bank[1], bank[3]), xs, S["nx_ready"], 6, S["nT_done"])
            for j in range(KC):
                last = mm(quarter(bank[2], j), xs[:, P * j:P * (j + 1)], Cn[:, :], start=True, stop=True)
            last.then_inc(S["nm_done"], 1)
            columns_halves((bank[4], bank[0]), xT, WsT, S["nT_ready"], 4, None, None, None)
            pe.wait_ge(S["nm_ready"], 1)
            for h in range(2):
                columns_by((bank[4], bank[0]), nmT, WnT, h, range(KC), None, KC - 1).then_inc(S["l3_done"], 1)

        @block.vector
        def _(dve):
            v = nc.vector
            chain = hop(dve, "dve_chain")
            norms = [0]

            def out_halves(dst, banks, done, before, signal):
                for h in range(2):
                    dve.wait_ge(done, before + h + 1)
                    v.tensor_copy(half(dst, h), banks[h][:, 0:D // 2]).then_inc(signal, 1)

            xT_flat = xT[:, :, :].rearrange("p c n -> p (c n)")

            def bank_statistics(banks, signal):
                for h in range(2):
                    dve.wait_ge(signal, h + 1)
                    chain(v.bn_stats(stats[:, h, :], banks[h][:, 0:D // 2]))
                return stats.rearrange("p h s -> p (h s)")

            def residual(banks, extra, signal):
                for h in range(2):
                    dve.wait_ge(signal, h + 1)
                    chain(v.tensor_tensor(half(y, h), banks[h][:, 0:D // 2], half(extra, h), ALU.add))
                    chain(v.bn_stats(stats[:, h, :], half(y, h)))
                return stats.rearrange("p h s -> p (h s)")

            def statistics(x):
                chain(v.bn_stats(stats[:, 0, :], x))
                return stats[:, 0, :]

            def halves(op, dst, src, signal):
                for h in range(2):
                    op(half(dst, h), src[h][:, 0:D // 2] if isinstance(src, tuple) else half(src, h), h).then_inc(signal, 1)

            def norm(src, dst, signal, st=None):
                norms[0] += 1
                chain(v.bn_aggr(mv[:, :], statistics(src) if st is None else st))
                v.tensor_scalar(mv[:, 1:2], mv[:, 1:2], EPS, None, ALU.add).then_inc(S["stat_ready"], 1)
                dve.wait_ge(S["rstd_ready"], norms[0])
                halves(lambda d, x, h: v.tensor_scalar(d, x, mv[:, 0:1], rstd[:, 0:1], ALU.subtract, ALU.mult), dst, src, signal)

            def norm_gain(src, dst, gain, plus, signal, st):
                norms[0] += 1
                chain(v.bn_aggr(mv[:, :], st))
                v.tensor_scalar(mv[:, 1:2], mv[:, 1:2], EPS, None, ALU.add).then_inc(S["stat_ready"], 1)
                if isinstance(src, tuple):
                    for h in range(2):
                        step = v.scalar_tensor_tensor(out=half(y, h), in0=src[h][:, 0:D // 2], scalar=mv[:, 0:1], in1=half(gain, h),
                                                      op0=ALU.subtract, op1=ALU.mult)
                    chain(step)
                    src = y[:, :]
                else:
                    chain(v.scalar_tensor_tensor(out=src, in0=src, scalar=mv[:, 0:1], in1=gain, op0=ALU.subtract, op1=ALU.mult))
                dve.wait_ge(S["rstd_ready"], norms[0])
                if signal is None:
                    chain(v.scalar_tensor_tensor(out=dst, in0=src, scalar=rstd[:, 0:1], in1=plus, op0=ALU.mult, op1=ALU.add))
                    return
                halves(lambda d, x, h: v.scalar_tensor_tensor(out=d, in0=x, scalar=rstd[:, 0:1], in1=half(plus, h),
                                                              op0=ALU.mult, op1=ALU.add), dst, src, signal)

            def r(name):
                return rows[:, slot[name], :]

            dve.wait_ge(S["consts"], 3)
            v.tensor_scalar(ident[:, :], iota_row[:, :], iota_col[:, 0:1], None, ALU.is_equal).then_inc(S["ident_ready"], 1)
            chain(v.memset(tiny[:, :], TINY))
            chain(v.memset(ones[:, :], 1.0))
            dve.wait_ge(S["x_transposed"], 1)
            v.tensor_copy(xT[:, :, :].rearrange("p c n -> p (c n)"), bank[1][:, :]).then_inc(S["xT_ready"], 1)
            dve.wait_ge(S["ids_in"], 32)
            for ids, one in ((dcol, Dbf), (scol, Sbf)):
                v.tensor_tensor(one, ids[:, :].unsqueeze(2).to_broadcast([P, ET, N]),
                                iota_row[:, :].unsqueeze(1).to_broadcast([P, ET, N]), ALU.is_equal).then_inc(S["onehot_bf"], 1)
            def node_hot(one, ids):
                v.tensor_scalar(one[:, :].rearrange("n (t p) -> n t p", p=P), ids.rearrange("n (p t) -> n t p", p=P),
                                iota_col[:, 0:1], None, ALU.is_equal).then_inc(S["st_ready"], 1)

            dve.wait_ge(S["bc_ready"], 1)
            node_hot(ST, src_bc)
            dve.wait_ge(S["ct_done"], 1)
            v.tensor_copy(CTs[:, :], bank[5][:, 0:N]).then_inc(S["ct_read"], 1)
            dve.wait_ge(S["ct_read"], 1)
            chain(v.tensor_scalar(mask[:, :], CTs[:, :], 1.0, None, ALU.min))
            dve.wait_ge(S["scores_done"], 1)
            for o in range(2):
                v.tensor_tensor(attn[:, o], (bank[1] if o == 0 else bank[7])[:, :].rearrange("p (j n) -> p j n", j=KC),
                                mask[:, :].unsqueeze(1).to_broadcast([P, KC, N]), ALU.mult).then_inc(S["scores_read"], 1)
            dve.wait_ge(S["scores_read"], 2)
            by_node = attn.rearrange("p o j n -> p n (o j)")
            top = small_n[:, 0, :]
            chain(v.tensor_reduce(top, by_node, AX.X, ALU.max))
            for o in range(2):
                v.tensor_tensor(attn[:, o], attn[:, o], top.unsqueeze(1).to_broadcast([P, KC, N]), ALU.subtract).then_inc(S["s_centred"], 1)
            dve.wait_ge(S["v_done"], 1)
            dve.wait_ge(row_out, 1)
            v.tensor_tensor(v_sb, bank[4][:, :], r("L0_gnn_bv"), ALU.add).then_inc(S["v_ready"], 1)
            dve.wait_ge(S["exp_done"], 2)
            total = small_n[:, 1, :]
            chain(v.tensor_reduce(total, by_node, AX.X, ALU.add))
            chain(v.reciprocal(total, total))
            for o in range(2):
                v.tensor_tensor(attn[:, o], attn[:, o], total.unsqueeze(1).to_broadcast([P, KC, N]), ALU.mult).then_inc(S["attn_ready"], 1)
            dve.wait_ge(row_out, 8)
            v.tensor_tensor(xw[:, :], xs[:, :], r("L0_gnn_bo"), ALU.add).then_inc(S["xw_ready"], 1)
            dve.wait_ge(S["ao_done"], 1)
            for h in range(2):
                v.tensor_copy(half(aoT.rearrange("p c n -> p (c n)"), h), half(bank[2], h)).then_inc(S["ao_ready"], 1)
            chain(v.tensor_tensor(xb, xs[:, :], r("L0_gnn_be2"), ALU.add))
            dve.wait_ge(S["bc_ready"], 2)
            node_hot(DT, dst_bc)
            st = bank_statistics((bank[3], bank[4]), S["wo_done"])
            norm_gain((bank[3], bank[4]), y[:, :], r("L0_gnn_g1"), r("L0_gnn_be1"), S["nx_ready"], st)
            out_halves(xT_flat, (bank[1], bank[2]), S["nT_done"], 0, S["nT_ready"])
            dve.wait_ge(S["nx_ready"], 2)
            chain(v.tensor_tensor(xw[:, :], y[:, :], r("L0_gnn_b2"), ALU.add))
            dve.wait_ge(S["wc_in"], 32)
            chain(v.tensor_copy(Chi[:, :], Wc_raw[:, :]))
            v.tensor_tensor(Clo[:, :], Wc_raw[:, :], Chi[:, :].bitcast(F32), ALU.subtract).then_inc(S["c_split"], 1)
            chain(v.tensor_reduce(small[:, 0:1], CTs[:, :], AX.X, ALU.add))
            v.tensor_scalar(small[:, 1:2], small[:, 0:1], 1.0, None, ALU.add).then_inc(S["deg_ready"], 1)
            chain(v.tensor_scalar(small[:, 3:4], small[:, 0:1], 1.0, None, ALU.max))
            chain(v.reciprocal(small[:, 4:5], small[:, 3:4]))
            v.tensor_scalar(Cn[:, :], CTs[:, :], small[:, 4:5], None, ALU.mult).then_inc(S["graphT_ready"], 1)
            chain(v.tensor_tensor(mask[:, :], CTs[:, :], ident[:, :], ALU.add))
            dve.wait_ge(S["dinv_ready"], 1)
            v.tensor_scalar(Ahat[:, :], mask[:, :], small[:, 2:3], None, ALU.mult).then_inc(S["graphT_ready"], 1)
            dve.wait_ge(S["graphT_done"], 1)
            v.tensor_scalar(Ahat[:, :], bank[7][:, 0:N], small[:, 2:3], None, ALU.mult).then_inc(S["graph_ready"], 1)
            v.tensor_copy(Cn[:, :], bank[7][:, N:2 * N]).then_inc(S["graph_ready"], 1)
            for i in range(4):
                dve.wait_ge(S["w1_hi"], i + 1)
                v.tensor_tensor(W1lo[:, 2 * i:2 * i + 2, :], W1ab[:, 2 * i:2 * i + 2, :],
                                W1hi[:, 2 * i:2 * i + 2, :].bitcast(F32), ALU.subtract).then_inc(S["w1_lo"], 1)
            st = residual((bank[3], bank[1]), xw, S["f2_done"])
            norm_gain(y[:, :], y[:, :], r("L0_gnn_g2"), xb, None, st)
            norm(y[:, :], xs[:, :], S["nx_ready"])
            xh, xl = (x.rearrange("p c n -> p (c n)") for x in (xhi, xlo))
            xs_banks = (bank[1], bank[7])
            out_halves(xh, xs_banks, S["nT_done"], 2, S["xs_hi"])
            for h in range(2):
                dve.wait_ge(S["xs_hi"], h + 1)
                v.tensor_tensor(half(xl, h), xs_banks[h][:, 0:D // 2], half(xh, h).bitcast(F32), ALU.subtract).then_inc(S["xs_lo"], 1)
            out_halves(xT_flat, xs_banks, S["nT_done"], 2, S["nT_ready"])
            dve.wait_ge(S["ab_done"], 1)
            v.tensor_copy(Ahi, bank[2][:, :]).then_inc(S["ab_ready"], 1)
            dve.wait_ge(S["ab_ready"], 1)
            v.tensor_tensor(Alo, bank[2][:, :], Ahi.bitcast(F32), ALU.subtract).then_inc(S["ab_ready"], 1)
            dve.wait_ge(S["ab_done"], 2)
            for h in range(2):
                v.tensor_copy(half(Bhi, h), half(bank[4], h)).then_inc(S["ab_ready"], 1)
                dve.wait_ge(S["ab_ready"], 2 * h + 3)
                v.tensor_tensor(half(Blo, h), half(bank[4], h), half(Bhi, h).bitcast(F32), ALU.subtract).then_inc(S["ab_ready"], 1)

            def z1_out(g, j):
                dve.wait_ge(S["z1_done"], units(g, j) + 1)
                if j == 0 and g >= 2:
                    dve.wait_ge(S["h_lo"], 2 * (g - 1))
                c = col["L1_gnn_b1"] + j
                v.tensor_scalar(z1(g)[:, j, :], ST1[units(g, j) % 3][:, :], cols[:, c:c + 1], None, ALU.add).then_inc(S["z1_read"], 1)

            def z1_out_half(h, j):
                u = KC * h + j
                dve.wait_ge(S["z1_done"], u + 1)
                c = col["L1_gnn_b1"] + j
                v.tensor_scalar(z1(0)[:, j, GE // 2 * h:GE // 2 * (h + 1)], ST1[u % 3][:, 0:GE // 2], cols[:, c:c + 1], None,
                                ALU.add).then_inc(S["z1_read"], 1)

            def z2_out(g, t):
                dve.wait_ge(S["z2_done"], GT * g + t + 1)
                if t == 0 and g == G - 1:
                    dve.wait_ge(S["h_lo"], 2 * G)
                elif t == 0 and g >= 2:
                    dve.wait_ge(S["m_lo"], 2 * (g - 1))
                v.tensor_tensor(z2(g)[:, t, :], ST2[t][:, :], r("L1_gnn_b2"), ALU.add).then_inc(S["z2_read"], 1)

            def h_product(g, h):
                e = slice(GE // 2 * h, GE // 2 * (h + 1))
                dve.wait_ge(S["tanh1"], 2 * g + h + 1)
                v.tensor_tensor(z1(g)[:, :, e], z1(g)[:, :, e], T1[:, :, e], ALU.mult).then_inc(S["h_mul"], 1)

            def h_high(g, h):
                e = slice(GE // 2 * h, GE // 2 * (h + 1))
                dve.wait_ge(S["h_mul"], 2 * g + h + 1)
                if g >= 2:
                    dve.wait_ge(S["z2_done"], GT * (g - 1))
                v.tensor_copy(Hhi[:, g % 2, :, e], z1(g)[:, :, e]).then_inc(S["h_hi"], 1)
                if g == 0:
                    dve.wait_ge(S["h_hi"], h + 1)
                    v.tensor_tensor(Hlo[:, 0, :, e], z1(0)[:, :, e], Hhi[:, 0, :, e].bitcast(F32), ALU.subtract).then_inc(S["h_lo"], 1)

            def m_product(g, h):
                t = slice(2 * h, 2 * (h + 1))
                dve.wait_ge(S["tanh2"], 2 * g + h + 1)
                v.tensor_tensor(z2(g)[:, t, :], z2(g)[:, t, :], T2[:, t, :], ALU.mult).then_inc(S["m_mul"], 1)

            def one_hot(g):
                if 1 <= g < G - 2:
                    dve.wait_ge(S["agg_done"], g)
                dst, signal = {G - 2: (Dg6, S["oh_late"]), G - 1: (Dg7, S["oh_late"])}.get(g, (Dg[:, :, :], S["m_oh"]))
                v.tensor_tensor(dst, dcol[:, GT * g:GT * (g + 1)].unsqueeze(2).to_broadcast([P, GT, N]),
                                iota_row[:, :].unsqueeze(1).to_broadcast([P, GT, N]), ALU.is_equal).then_inc(signal, 1)

            def m_high(g, h):
                t = slice(2 * h, 2 * (h + 1))
                dve.wait_ge(S["m_mul"], 2 * g + h + 1)
                v.tensor_copy(Mhi[:, t, :], z2(g)[:, t, :]).then_inc(S["m_hi"], 1)

            def h_out(g, h):
                h_product(g, h)
                h_high(g, h)

            for i in range(2 * KC):
                z1_out_half(i // KC, i % KC)
            for j in range(3):
                z1_out(1, j)
            h_out(0, 0)
            z1_out(1, 3)
            h_out(0, 1)
            z1_out(2, 0)
            z2_out(0, 0)
            z2_out(0, 1)
            z1_out(2, 1)
            z2_out(0, 2)
            h_out(1, 0)
            z2_out(0, 3)
            h_out(1, 1)
            z1_out(2, 2)
            z1_out(2, 3)
            for s in range(LAG2 + 1, G):
                gh, g2, gm = s - 1, s - LAG2, s - 1 - LAG2
                for j in range(KC - 1):
                    z1_out(s, j)
                z2_out(g2, 0)
                z2_out(g2, 1)
                z1_out(s, KC - 1)
                h_out(gh, 0)
                h_out(gh, 1)
                z2_out(g2, 2)
                m_product(gm, 0)
                m_product(gm, 1)
                z2_out(g2, 3)
                one_hot(gm)
                m_high(gm, 0)
                m_high(gm, 1)
            def late_out(g, t):
                z2_out(g, t)
                dve.wait_ge(S["z2_read"], GT * g + t + 1)
                if g == G - 1 and t == 0:
                    dve.wait_ge(S["m_mul"], 2 * (G - 2))
                v.tensor_scalar((T1 if g == G - 2 else T2)[:, t, :], z2(g)[:, t, :], TOP, None, ALU.min).then_inc(S["late_top"], 1)

            def late_product(g, t, tiles):
                part = slice(t, t + tiles)
                dve.wait_ge(S["late_tanh"], GT * (g - G + 2) + t + tiles)
                v.tensor_tensor(z2(g)[:, part, :], z2(g)[:, part, :], (T1 if g == G - 2 else T2)[:, part, :],
                                ALU.mult).then_inc(S["late_mul"], tiles)

            h_out(G - 1, 0)
            h_out(G - 1, 1)
            dve.wait_ge(S["h_mul"], 2 * G)
            for t in range(GT - 1):
                late_out(G - 2, t)
            m_product(G - 3, 0)
            late_out(G - 2, GT - 1)
            m_product(G - 3, 1)
            one_hot(G - 3)
            m_high(G - 3, 0)
            m_high(G - 3, 1)
            late_out(G - 1, 0)
            one_hot(G - 2)
            late_out(G - 1, 1)
            one_hot(G - 1)
            late_out(G - 1, 2)
            late_product(G - 2, 0, 2)
            late_out(G - 1, 3)
            late_product(G - 2, 2, 2)
            for t in range(GT):
                late_product(G - 1, t, 1)
            dve.wait_ge(S["agg_done"], G - 1)
            for h in range(2):
                v.tensor_copy(half(agg_sb, h), half(AGG, h)).then_inc(S["agg_ready"], 1)
            dve.wait_ge(row_out, 15)
            v.tensor_tensor(xw[:, :], xs[:, :], r("L1_gnn_b4"), ALU.add).then_inc(S["xw_ready"], 1)
            out_halves(aggT.rearrange("p c n -> p (c n)"), (bank[1], bank[3]), S["aggT_done"], 0, S["aggT_ready"])
            dve.wait_ge(S["ux_done"], 3)
            c = col["L1_gnn_b3"]
            v.tensor_tensor(chunks(ux, KC), bank[7][:, :].rearrange("p (j n) -> p j n", j=KC),
                            cols[:, c:c + KC].unsqueeze(2).to_broadcast([P, KC, N]), ALU.add).then_inc(S["ux_ready"], 1)
            chain(v.tensor_tensor(xb_late, xs[:, :], r("L1_gnn_beta"), ALU.add))
            dve.wait_ge(S["ux_ready"], 1)
            for h in range(2):
                dve.wait_ge(S["u_done"], h + 1)
                chain(v.tensor_tensor(half(zu, h), bank[5 if h else 2][:, 0:D // 2], half(ux, h), ALU.add))
                v.tensor_scalar(half(tu, h), half(zu, h), TOP, None, ALU.min).then_inc(S["zu_ready"], 1)
            for h in range(2):
                dve.wait_ge(S["u_act"], h + 1)
                v.tensor_tensor(half(uT.rearrange("p c n -> p (c n)"), h), half(zu, h), half(tu, h), ALU.mult).then_inc(S["u_ready"], 1)
            st = bank_statistics((bank[1], bank[5]), S["o_done"])
            norm_gain((bank[1], bank[5]), y[:, :], r("L1_gnn_gamma"), xb_late, None, st)
            norm(y[:, :], xs[:, :], S["nx_ready"])
            dve.wait_ge(S["g0_done"], 1)
            v.tensor_copy(xT[:, :, :].rearrange("p c n -> p (c n)"), bank[2][:, :]).then_inc(S["g0_ready"], 1)
            dve.wait_ge(S["nx_ready"], 6)
            v.tensor_tensor(xw[:, :], xs[:, :], r("L2_gnn_b2"), ALU.add).then_inc(S["xw_ready"], 1)
            dve.wait_ge(S["g1_done"], 1)
            v.tensor_scalar(r1g, bank[3][:, 0:HID2], 0.0, None, ALU.max).then_inc(S["g1_ready"], 1)
            dve.wait_ge(S["g2_done"], 1)
            v.tensor_copy(p1g, bank[4][:, 0:N]).then_inc(S["g2_ready"], 1)
            norm((bank[5], bank[6]), xs[:, :], S["nx_ready"], bank_statistics((bank[5], bank[6]), S["g3_done"]))
            out_halves(xT_flat, (bank[1], bank[3]), S["nT_done"], 4, S["nT_ready"])
            dve.wait_ge(S["nm_done"], 1)
            v.tensor_copy(nmT.rearrange("p c n -> p (c n)"), bank[2][:, :]).then_inc(S["nm_ready"], 1)
            dve.wait_ge(S["nx_ready"], 8)
            chain(v.tensor_tensor(xs[:, :], xs[:, :], r("L3_gnn_beta"), ALU.add))
            st = bank_statistics((bank[4], bank[0]), S["l3_done"])
            norm_gain((bank[4], bank[0]), y[:, :], r("L3_gnn_gamma"), xs[:, :], None, st)
            norm(y[:, :], y[:, :], S["y_final"])


def kernel(**inputs):
    import numpy as np
    import concourse.bacc as bacc
    from concourse import mybir as mb
    from concourse.bass_utils import run_bass_kernel_spmd as run

    nc = bacc.Bacc("TRN2", target_bir_lowering=False, num_devices=1)
    arrays, args = {}, {}
    for name, value in inputs.items():
        v = np.ascontiguousarray(value)
        arrays[f"in_{name}"] = v
        args[name] = nc.dram_tensor(f"in_{name}", v.shape, mb.dt.from_np(v.dtype), kind="ExternalInput").ap()
    out = nc.dram_tensor("out_0", (N, D), F32, kind="ExternalOutput").ap()
    gnn_kernel(nc, args, out)
    r = run(nc, [arrays], core_ids=[0])
    return r.results[0]["out_0"]
```
